# Optimizing a Trainium2 kernel written in Bass

```python
import numpy as np
import jax
import jax.numpy as jnp

def _softmax(x, axis=-1):
    return jax.nn.softmax(x, axis=axis)

def _gelu(x):
    return jax.nn.gelu(x, approximate=True)

def _silu(x):
    return jax.nn.silu(x)

def _sigmoid(x):
    return jax.nn.sigmoid(x)

def _layernorm(x, axis=-1, eps=1e-05):
    m = jnp.mean(x, axis=axis, keepdims=True)
    v = jnp.var(x, axis=axis, keepdims=True)
    return (x - m) / jnp.sqrt(v + eps)

def _scatter_add(tgt, idx, src, axis=0):
    return tgt.at[idx].add(src)

def _segment_sum(src, seg, n):
    return jax.ops.segment_sum(src, seg, n)
kernel_name = 'mk_adaln_d2_jaxref_r8_de5126'

def setup_inputs(seed: int=0):
    np.random.seed(seed)
    _w = jnp.asarray

    def _L0_attn_setup():
        import jax, jax.numpy as jnp
        import numpy as np
        D_MODEL = 128
        N_HEADS = 16
        HIDDEN = max(8, D_MODEL // 2)
        EPS = 1e-12
        key = jax.random.key(seed)
        ks = jax.random.split(key, 12)
        s = 0.02
        inp = {'x': jax.random.normal(ks[0], (8, 128, D_MODEL), dtype=jnp.float32), 'Wq': jax.random.normal(ks[1], (D_MODEL, D_MODEL), dtype=jnp.float32) * s, 'bq': jnp.zeros((D_MODEL,), dtype=jnp.float32), 'Wk': jax.random.normal(ks[2], (D_MODEL, D_MODEL), dtype=jnp.float32) * s, 'bk': jnp.zeros((D_MODEL,), dtype=jnp.float32), 'Wv': jax.random.normal(ks[3], (D_MODEL, D_MODEL), dtype=jnp.float32) * s, 'bv': jnp.zeros((D_MODEL,), dtype=jnp.float32), 'Wo': jax.random.normal(ks[4], (D_MODEL, D_MODEL), dtype=jnp.float32) * s, 'bo': jnp.zeros((D_MODEL,), dtype=jnp.float32), 'g': jnp.zeros((N_HEADS,), dtype=jnp.float32), 'Wg1': jax.random.normal(ks[5], (HIDDEN, D_MODEL), dtype=jnp.float32) * s, 'bg1': jnp.zeros((HIDDEN,), dtype=jnp.float32), 'Wg2': jax.random.normal(ks[6], (N_HEADS, HIDDEN), dtype=jnp.float32) * s, 'bg2': jnp.zeros((N_HEADS,), dtype=jnp.float32)}
        return inp
    _L0_attn_in = _L0_attn_setup()

    def _L0_ffn_setup():
        import jax, jax.numpy as jnp
        import numpy as np
        D_MODEL = 128
        E = 4
        MIN_E = 1
        TH_LO = 0.5
        TH_HI = 2.0
        key = jax.random.key(seed)
        ks = jax.random.split(key, 12)
        B, N, D, H = (4, 256, D_MODEL, 2 * D_MODEL)
        s = 0.02
        return {'x': jax.random.normal(ks[0], (B, N, D), dtype=jnp.float32), 'gate_w': jax.random.normal(ks[1], (D, E), dtype=jnp.float32) * s, 'gate_b': jnp.zeros((E,), dtype=jnp.float32), 'dp_w1': jax.random.normal(ks[2], (D, D // 2), dtype=jnp.float32) * s, 'dp_b1': jnp.zeros((D // 2,), dtype=jnp.float32), 'dp_w2': jax.random.normal(ks[3], (D // 2, 1), dtype=jnp.float32) * s, 'dp_b2': jnp.zeros((1,), dtype=jnp.float32), 'ew1': jax.random.normal(ks[4], (E, D, H), dtype=jnp.float32) * s, 'eb1': jnp.zeros((E, H), dtype=jnp.float32), 'ew2': jax.random.normal(ks[5], (E, H, D), dtype=jnp.float32) * s, 'eb2': jnp.zeros((E, D), dtype=jnp.float32)}
    _L0_ffn_in = _L0_ffn_setup()
    _L0_c = _w((lambda *s: np.random.randn(*s).astype(np.float32) * 0.05)(32, 128))
    _L0_wmod = _w((lambda *s: np.random.randn(*s).astype(np.float32) * 0.05)(128, 6 * 128) * 128 ** (-0.5))

    def _L1_attn_setup():
        import jax, jax.numpy as jnp
        import numpy as np
        B, S, D, H = (2, 256, 128, 16)
        MASK_VAL = -50000.0
        key = jax.random.key(seed)
        k1, k2, k3, k4 = jax.random.split(key, 4)
        s = 1.0 / np.sqrt(D)
        return {'x': jax.random.normal(k1, (B, S, D), dtype=jnp.float32), 'Wq': jax.random.normal(k2, (D, D), dtype=jnp.float32) * s, 'Wkv': jax.random.normal(k3, (D, 2 * D), dtype=jnp.float32) * s, 'Wo': jax.random.normal(k4, (D, D), dtype=jnp.float32) * s}
    _L1_attn_in = _L1_attn_setup()

    def _L1_ffn_setup():
        import jax, jax.numpy as jnp
        import numpy as np
        B, T, C, E, K, H = (4, 128, 128, 8, 2, 512)
        key = jax.random.key(seed)
        ks = jax.random.split(key, 7)
        s = 0.02
        return {'x': jax.random.normal(ks[0], (B, T, C), dtype=jnp.float32), 'Wg': jax.random.normal(ks[1], (C, E), dtype=jnp.float32) * s, 'bg': jnp.zeros((E,), dtype=jnp.float32), 'W1': jax.random.normal(ks[2], (E, C, H), dtype=jnp.float32) * s, 'b1': jnp.zeros((E, H), dtype=jnp.float32), 'W2': jax.random.normal(ks[3], (E, H, C), dtype=jnp.float32) * s, 'b2': jnp.zeros((E, C), dtype=jnp.float32)}
    _L1_ffn_in = _L1_ffn_setup()
    _L1_c = _w((lambda *s: np.random.randn(*s).astype(np.float32) * 0.05)(32, 128))
    _L1_wmod = _w((lambda *s: np.random.randn(*s).astype(np.float32) * 0.05)(128, 6 * 128) * 128 ** (-0.5))
    _d = {'L0_attn_x': _L0_attn_in['x'], 'L0_attn_Wq': _L0_attn_in['Wq'], 'L0_attn_bq': _L0_attn_in['bq'], 'L0_attn_Wk': _L0_attn_in['Wk'], 'L0_attn_bk': _L0_attn_in['bk'], 'L0_attn_Wv': _L0_attn_in['Wv'], 'L0_attn_bv': _L0_attn_in['bv'], 'L0_attn_Wo': _L0_attn_in['Wo'], 'L0_attn_bo': _L0_attn_in['bo'], 'L0_attn_g': _L0_attn_in['g'], 'L0_attn_Wg1': _L0_attn_in['Wg1'], 'L0_attn_bg1': _L0_attn_in['bg1'], 'L0_attn_Wg2': _L0_attn_in['Wg2'], 'L0_attn_bg2': _L0_attn_in['bg2'], 'L0_ffn_gate_w': _L0_ffn_in['gate_w'], 'L0_ffn_gate_b': _L0_ffn_in['gate_b'], 'L0_ffn_dp_w1': _L0_ffn_in['dp_w1'], 'L0_ffn_dp_b1': _L0_ffn_in['dp_b1'], 'L0_ffn_dp_w2': _L0_ffn_in['dp_w2'], 'L0_ffn_dp_b2': _L0_ffn_in['dp_b2'], 'L0_ffn_ew1': _L0_ffn_in['ew1'], 'L0_ffn_eb1': _L0_ffn_in['eb1'], 'L0_ffn_ew2': _L0_ffn_in['ew2'], 'L0_ffn_eb2': _L0_ffn_in['eb2'], 'L0_c': _L0_c, 'L0_wmod': _L0_wmod, 'L1_attn_Wq': _L1_attn_in['Wq'], 'L1_attn_Wkv': _L1_attn_in['Wkv'], 'L1_attn_Wo': _L1_attn_in['Wo'], 'L1_ffn_Wg': _L1_ffn_in['Wg'], 'L1_ffn_bg': _L1_ffn_in['bg'], 'L1_ffn_W1': _L1_ffn_in['W1'], 'L1_ffn_b1': _L1_ffn_in['b1'], 'L1_ffn_W2': _L1_ffn_in['W2'], 'L1_ffn_b2': _L1_ffn_in['b2'], 'L1_c': _L1_c, 'L1_wmod': _L1_wmod}
    _x0 = _d['L0_attn_x']
    _d['L0_attn_x'] = jax.random.normal(jax.random.fold_in(jax.random.key(seed), 1), (32, 256, 128), dtype=_x0.dtype)
    del _x0
    return _d

def reference(L0_attn_x, L0_attn_Wq, L0_attn_bq, L0_attn_Wk, L0_attn_bk, L0_attn_Wv, L0_attn_bv, L0_attn_Wo, L0_attn_bo, L0_attn_g, L0_attn_Wg1, L0_attn_bg1, L0_attn_Wg2, L0_attn_bg2, L0_ffn_gate_w, L0_ffn_gate_b, L0_ffn_dp_w1, L0_ffn_dp_b1, L0_ffn_dp_w2, L0_ffn_dp_b2, L0_ffn_ew1, L0_ffn_eb1, L0_ffn_ew2, L0_ffn_eb2, L0_c, L0_wmod, L1_attn_Wq, L1_attn_Wkv, L1_attn_Wo, L1_ffn_Wg, L1_ffn_bg, L1_ffn_W1, L1_ffn_b1, L1_ffn_W2, L1_ffn_b2, L1_c, L1_wmod):

    def _L0_attn_ref(x, Wq, bq, Wk, bk, Wv, bv, Wo, bo, g, Wg1, bg1, Wg2, bg2):
        import jax, jax.numpy as jnp
        import numpy as np
        D_MODEL = 128
        N_HEADS = 16
        HIDDEN = max(8, D_MODEL // 2)
        EPS = 1e-12
        B, T, D = x.shape
        H, dk = (N_HEADS, D // N_HEADS)

        def proj(W, b):
            return (x @ W.T + b).reshape(B, T, H, dk).transpose(0, 2, 1, 3)
        Q = proj(Wq, bq)
        K = proj(Wk, bk)
        V = proj(Wv, bv)
        Qn = Q / jnp.maximum(jnp.linalg.norm(Q, axis=-1, keepdims=True), EPS)
        Kn = K / jnp.maximum(jnp.linalg.norm(K, axis=-1, keepdims=True), EPS)
        scores = jnp.einsum('bhqd,bhkd->bhqk', Qn, Kn) / jnp.sqrt(jnp.float32(dk))
        attn = jax.nn.softmax(scores, axis=-1)
        head_outs = jnp.einsum('bhqk,bhkd->bhqd', attn, V)
        gate_static = jax.nn.sigmoid(g)[None, :, None, None]
        h = jax.nn.gelu(x @ Wg1.T + bg1, approximate=False)
        gate_logits = (h @ Wg2.T + bg2).mean(axis=1)
        gate_dynamic = jax.nn.sigmoid(gate_logits)[:, :, None, None]
        head_outs = head_outs * (gate_static * gate_dynamic)
        out = head_outs.transpose(0, 2, 1, 3).reshape(B, T, D)
        return out @ Wo.T + bo

    def _L0_ffn_ref(x, gate_w, gate_b, dp_w1, dp_b1, dp_w2, dp_b2, ew1, eb1, ew2, eb2):
        import jax, jax.numpy as jnp
        import numpy as np
        D_MODEL = 128
        E = 4
        MIN_E = 1
        TH_LO = 0.5
        TH_HI = 2.0
        B, N, D = x.shape
        xf = x.reshape(B * N, D)
        T = B * N
        h = jax.nn.relu(xf @ dp_w1 + dp_b1)
        entropy = jax.nn.softplus(h @ dp_w2 + dp_b2)[:, 0]
        norm = jnp.clip((entropy - TH_LO) / (TH_HI - TH_LO), 0.0, 1.0)
        k_tok = jnp.clip(jnp.round(MIN_E + norm * (E - MIN_E)).astype(jnp.int32), MIN_E, E)
        logits = xf @ gate_w + gate_b
        top_logits, top_idx = jax.lax.top_k(logits, E)
        pos = jnp.arange(E)
        sel = pos[None, :] < k_tok[:, None]
        masked = jnp.where(sel, top_logits, -jnp.inf)
        w_top = jax.nn.softmax(masked, axis=-1)
        dense_w = jnp.zeros((T, E), dtype=xf.dtype).at[jnp.arange(T)[:, None], top_idx].set(w_top)
        hid = jax.nn.relu(jnp.einsum('td,edh->teh', xf, ew1) + eb1[None, :, :])
        y = jnp.einsum('teh,ehd->ted', hid, ew2) + eb2[None, :, :]
        out = jnp.einsum('te,ted->td', dense_w, y)
        return out.reshape(B, N, D)

    def _L1_attn_ref(x, Wq, Wkv, Wo):
        import jax, jax.numpy as jnp
        import numpy as np
        B, S, D, H = (2, 256, 128, 16)
        MASK_VAL = -50000.0
        b, sl, d = x.shape
        h = H
        hd = d // h
        scale = hd ** (-0.5)
        q = x @ Wq
        kv = x @ Wkv
        k, v = jnp.split(kv, 2, axis=-1)
        q = q.reshape(b, sl, h, hd).transpose(0, 2, 1, 3)
        k = k.reshape(b, sl, h, hd).transpose(0, 2, 1, 3)
        v = v.reshape(b, sl, h, hd).transpose(0, 2, 1, 3)
        dots = jnp.einsum('bhid,bhjd->bhij', q * scale, k)
        causal = jnp.tril(jnp.ones((sl, sl), dtype=bool))
        dots = jnp.where(causal, dots, MASK_VAL)
        attn = jax.nn.softmax(dots, axis=-1)
        out = jnp.einsum('bhij,bhjd->bihd', attn, v).reshape(b, sl, d)
        return out @ Wo

    def _L1_ffn_ref(x, Wg, bg, W1, b1, W2, b2):
        import jax, jax.numpy as jnp
        import numpy as np
        B, T, C, E, K, H = (4, 128, 128, 8, 2, 512)
        Bx, Tx, Cx = x.shape
        xf = x.reshape(Bx * Tx, Cx)
        N = xf.shape[0]
        gate = xf @ Wg + bg
        topv, topi = jax.lax.top_k(gate, K)
        probs = jax.nn.softmax(topv, axis=-1)
        comb = jnp.zeros((N, E), dtype=xf.dtype).at[jnp.arange(N)[:, None], topi].set(probs)
        h = jax.nn.relu(jnp.einsum('nc,ecf->nef', xf, W1) + b1)
        y = jnp.einsum('nef,efc->nec', h, W2) + b2
        out = jnp.einsum('nec,ne->nc', y, comb)
        return out.reshape(Bx, Tx, Cx)
    x = L0_attn_x
    mod = (_silu(L0_c) @ L0_wmod).reshape(L0_c.shape[0], 6, 1, -1)
    sa, ca, ga, sb, cb, gb = (mod[:, 0], mod[:, 1], mod[:, 2], mod[:, 3], mod[:, 4], mod[:, 5])
    ga = (2 * (ga >= 0) - 1) * jnp.maximum(jnp.abs(ga), 0.25)
    gb = (2 * (gb >= 0) - 1) * jnp.maximum(jnp.abs(gb), 0.25)
    h = _layernorm(x, axis=-1) * (1 + ca) + sa
    x = x + ga * _L0_attn_ref(h, L0_attn_Wq, L0_attn_bq, L0_attn_Wk, L0_attn_bk, L0_attn_Wv, L0_attn_bv, L0_attn_Wo, L0_attn_bo, L0_attn_g, L0_attn_Wg1, L0_attn_bg1, L0_attn_Wg2, L0_attn_bg2)
    h = _layernorm(x, axis=-1) * (1 + cb) + sb
    x = x + gb * _L0_ffn_ref(h, L0_ffn_gate_w, L0_ffn_gate_b, L0_ffn_dp_w1, L0_ffn_dp_b1, L0_ffn_dp_w2, L0_ffn_dp_b2, L0_ffn_ew1, L0_ffn_eb1, L0_ffn_ew2, L0_ffn_eb2)
    mod = (_silu(L1_c) @ L1_wmod).reshape(L1_c.shape[0], 6, 1, -1)
    sa, ca, ga, sb, cb, gb = (mod[:, 0], mod[:, 1], mod[:, 2], mod[:, 3], mod[:, 4], mod[:, 5])
    ga = (2 * (ga >= 0) - 1) * jnp.maximum(jnp.abs(ga), 0.25)
    gb = (2 * (gb >= 0) - 1) * jnp.maximum(jnp.abs(gb), 0.25)
    h = _layernorm(x, axis=-1) * (1 + ca) + sa
    x = x + ga * _L1_attn_ref(h, L1_attn_Wq, L1_attn_Wkv, L1_attn_Wo)
    h = _layernorm(x, axis=-1) * (1 + cb) + sb
    x = x + gb * _L1_ffn_ref(h, L1_ffn_Wg, L1_ffn_bg, L1_ffn_W1, L1_ffn_b1, L1_ffn_W2, L1_ffn_b2)
    return x

_drawn_inputs = setup_inputs


def setup_inputs(seed=0):
    import zlib

    import numpy as np

    out = dict(_drawn_inputs(seed))
    spreads = {'L0_attn_bq': (0.0, 0.8),
     'L0_attn_bk': (0.0, 0.8),
     'L0_attn_bv': (0.0, 0.8),
     'L0_attn_bo': (0.0, 0.306),
     'L0_attn_g': (0.0, 0.8),
     'L0_attn_bg1': (0.0, 0.8),
     'L0_attn_bg2': (0.0, 0.8),
     'L0_ffn_gate_b': (0.0, 0.348),
     'L0_ffn_dp_b1': (0.0, 0.1),
     'L0_ffn_eb1': (0.0, 0.8),
     'L0_ffn_eb2': (0.0, 0.319),
     'L1_ffn_bg': (0.0, 0.543),
     'L1_ffn_b1': (0.0, 0.8),
     'L1_ffn_b2': (0.0, 0.441)}
    factors = {'L0_attn_Wq': 8.0,
     'L0_attn_Wk': 8.0,
     'L0_attn_Wv': 8.0,
     'L0_attn_Wo': 8.0,
     'L0_attn_Wg1': 8.0,
     'L0_attn_Wg2': 8.0,
     'L0_ffn_ew1': 5.076,
     'L0_ffn_ew2': 3.889,
     'L1_ffn_Wg': 2.838,
     'L1_ffn_W1': 5.23,
     'L1_ffn_W2': 4.087}
    for name, (base, spread) in spreads.items():
        noise = np.random.default_rng([zlib.crc32(name.encode()), seed]).standard_normal(out[name].shape)
        drawn = base * np.exp(spread * noise) if base else spread * noise
        out[name] = jnp.asarray(drawn.astype(out[name].dtype))
    for name, factor in factors.items():
        out[name] = (out[name] * factor).astype(out[name].dtype)
    return out
```

```python
from contextlib import ExitStack

import concourse.bass as bass
from concourse import mybir

F32 = mybir.dt.float32
F16 = mybir.dt.float16
BF16 = mybir.dt.bfloat16
ALU = mybir.AluOpType
ACT = mybir.ActivationFunctionType
AX = mybir.AxisListType

B, T, D = 32, 256, 128
P = 128
TT = T // P
NT = B * TT
H, DH = 16, 8
HG = 4
NJ = H // HG
HID = 64
E0, F0 = 4, 2
E1, F1 = 8, 4
GT = 4
NG = NT // GT
LN_EPS = 1e-5
NORM_EPS = 1e-12
SCALE = DH ** -0.5
NEG = -1e30
MSHIFT = 256.0
CH = 8

import math
K_CUTS = [(math.log(math.exp(0.5 + 1.5 * (c - 1.0) / 3.0) - 1.0), op)
          for c, op in ((1.5, ALU.is_ge), (2.5, ALU.is_gt), (3.5, ALU.is_ge))]

SA, CA, GA, SB, CB, GB = range(6)
NX = [HID, E0 + HID, 0, E1]
NMOD = [(0, SA, CA), (0, SB, CB), (1, SA, CA), (1, SB, CB)]


def program(nc, a, out):
    ctx = ExitStack()
    with ctx:
        def sb(name, shape, dt=F32):
            return ctx.enter_context(nc.sbuf_tensor(name, shape, dt))

        def pb(name, shape, dt=F32):
            return ctx.enter_context(nc.psum_tensor(name, shape, dt))

        def sem(name):
            return ctx.enter_context(nc.semaphore(name))

        x_sb = sb("x_sb", [P, NT, D])
        hT = sb("hT", [P, NT * P])
        rows = sb("rows", [P, B, D])
        modT = [sb(f"modT{l}", [P, 6, B]) for l in range(2)]
        wqkv = [sb(f"wqkv{l}", [P, 3 * D]) for l in range(2)]
        wo = [sb(f"wo{l}", [P, D]) for l in range(2)]
        bqkv = sb("bqkv", [P, 3 * D])
        bo = sb("bo", [P, D])
        wx = [sb("wx0", [P, NX[0]]), sb("wx1", [P, NX[1]]), None, sb("wx3", [P, NX[3]])]
        bx = [sb("bx0", [P, NX[0]]), sb("bx1", [P, NX[1]]), None, sb("bx3", [P, NX[3]])]
        dpw2 = sb("dpw2", [P, HID])
        dpb2 = sb("dpb2", [P, 1])
        wg2 = sb("wg2", [HID, H])
        bg2 = sb("bg2", [B, H])
        gst = sb("gst", [B, H])
        w1 = [sb("w1_0", [P, E0, F0 * P]), sb("w1_1", [P, E1, F1 * P])]
        w2 = [sb("w2_0", [P, E0 * F0, D]), sb("w2_1", [P, E1 * F1, D])]
        b1 = [sb("b1_0", [P, E0 * F0]), sb("b1_1", [P, E1 * F1])]
        b2 = [sb("b2_0", [E0, D]), sb("b2_1", [E1, D])]
        logit = [sb("logit0", [P, NT, E0]), sb("logit1", [P, NT, E1])]
        comb = [sb("comb0", [P, NT, E0]), sb("comb1", [P, NT, E1])]
        zdp = sb("zdp", [P, NT, 1])
        gsum = sb("gsum", [HID, B])
        gateB = sb("gateB", [P, B, H])
        ident = sb("ident", [P, P])
        ident16 = sb("ident16", [P, P], F16)
        identb = sb("identb", [P, P], BF16)
        ones = sb("ones", [P, 1])
        maskT = sb("maskT", [P, P], BF16)
        maskQ = sb("maskQ", [P, P], BF16)
        cT = [sb(f"cT{l}", [P, B]) for l in range(2)]
        ce = [sb(f"ce{l}", [P, B]) for l in range(2)]
        pt = sb("pt", [P, 4, 2, 512])
        free = pt[:].rearrange("p a b c -> p (a b c)")
        wmod = [free[:, l * 6 * D:(l + 1) * 6 * D] for l in range(2)]
        graw, gsign, gmag = [free[0:B, 12 * D + n * 4 * D:12 * D + (n + 1) * 4 * D].rearrange(
            "p (n d) -> p n d", n=4) for n in range(3)]
        gl = sb("gl", [B, H])
        gs = sb("gs", [B, H])
        stats = sb("stats", [P, NT, 6])
        mean = sb("mean", [P, NT])
        rstd = sb("rstd", [P, NT])
        dev = sb("dev", [P, NT])
        mhalf = sb("mhalf", [P, 2 * TT * H])
        z = sb("z", [P, 2, TT, D])
        hcur = sb("hcur", [P, 2, T])
        xt = sb("xt", [P, 2, TT, HID + E0])
        rt = sb("rt", [P, NT, E1])
        rank = sb("rank", [P, NT, E1])
        rm = sb("rm", [P, NT, 1])
        kt = sb("kt", [P, NT, 1])
        ha = sb("ha", [P, T])
        qk = sb("qk", [P, 2, TT, D])
        sq = sb("sq", [P, 2, TT, D])
        n2 = sb("n2", [P, 2 * TT * H, 1])
        st = sb("st", [P, 2, TT * H, 4, DH], F16)
        qsT = sb("qsT", [P, 2, NJ, T], F16)
        ksT = sb("ksT", [P, 2, NJ, T], F16)
        vs = sb("vs", [P, 2, TT, H, 32])
        oT = sb("oT", [P, NJ, T])
        rs = sb("rs", [P, TT * H, 1])
        an = sb("an", [P, TT * H, DH])
        aT = sb("aT", [P, T])
        ao = sb("ao", [P, TT, D])
        mx = sb("mx", [P, TT, NJ, HG])
        hid = pt[:].rearrange("p (e a) b n -> p e (a b) n", e=2)
        ccur = [sb("ccur0", [P, 2, GT, E0]), sb("ccur1", [P, 2, GT, E1])]
        cTr = [sb("cTr0", [E0, GT * P]), sb("cTr1", [E1, GT * P])]
        acc = sb("acc", [P, GT, D])

        SP = [pb("SP0", [P, 2, 512]), pb("SP1", [P, 2, 512])]
        OP = pb("OP", [P, 2, 512])
        M = pb("M", [P, 2, 512])
        bank = [SP[0][:, 0, :], SP[0][:, 1, :], SP[1][:, 0, :], SP[1][:, 1, :],
                OP[:, 0, :], OP[:, 1, :], M[:, 0, :], M[:, 1, :]]

        g_dram = [nc.dram_tensor(f"g_dram{n}", (B, D), F32, kind="Internal").ap() for n in range(4)]
        gate_dram = nc.dram_tensor("gate_dram", (B, H), F32, kind="Internal").ap()

        phase_end = sem("phase_end")
        x_in, w_in, late_in = sem("x_in"), sem("w_in"), sem("late_in")
        row_out, row_in, gate_out, gate_in = sem("row_out"), sem("row_in"), sem("gate_out"), sem("gate_in")
        y_out = sem("y_out")
        masks = sem("masks")
        idents = sem("idents")
        silu_e, silu_r = sem("silu_e"), sem("silu_r")
        mod_mm, mod_cp, g_mm, g_fin = sem("mod_mm"), sem("mod_cp"), sem("g_mm"), sem("g_fin")
        gl_mm, gl_in, gl_exp, gl_fin = sem("gl_mm"), sem("gl_in"), sem("gl_exp"), sem("gl_fin")

        def sems(kind, n, names):
            return {k: sem(f"{kind}{n}_{k}") for k in names.split()}

        norm_s = [sems("norm", n, "var rstd z zT h hT x xin gelu gmm gsum rexp") for n in range(4)]
        att_s = [sems("att", l, "h proj n2 rn qkv stack sT sE mfill mred mrow score exp pv o oT an aT aE wo x")
                 for l in range(2)]
        exp_s = [sems("exp", l, "c cT cE hid relu y b2 acc done") for l in range(2)]

        block = ctx.enter_context(nc.Block())
        ENGINES = 5

        def phase(eng, n):
            eng.drain().then_inc(phase_end, 1)
            eng.wait_ge(phase_end, ENGINES * n)

        LOADS = [(wqkv[0], "wqkv0"), (wqkv[1], "wqkv1"), (wo[0], "wo0"), (wo[1], "wo1"),
                 (bqkv, "bqkv0"), (bo, "bo0"), (wx[0], "wx0"), (wx[1], "wx1"), (wx[3], "wx3"),
                 (bx[0], "bx0"), (bx[1], "bx1"), (bx[3], "bx3"), (dpw2, "dpw2"), (dpb2, "dpb2"),
                 (wg2, "wg2"), (bg2, "bg2"), (gst, "g"), (b1[0], "b1_0"), (b1[1], "b1_1"),
                 (b2[0], "b2_0"), (b2[1], "b2_1")]
        FIRST = [(cT[0], "cT0"), (cT[1], "cT1"), (wmod[0], "wmod0"), (wmod[1], "wmod1")]
        LATE = [(w1[0], "w1_0"), (w2[0], "w2_0"), (w1[1], "w1_1"), (w2[1], "w2_1")]

        @block.sync
        def _(sp):
            for dst, name in FIRST:
                sp.dma_start(dst[:, :], a[name]).then_inc(w_in, 16)
            xd = a["x"].rearrange("b (t p) d -> p (b t) d", p=P)
            for i in range(8):
                sp.dma_start(x_sb[:, i * 8:i * 8 + 8, :], xd[:, i * 8:i * 8 + 8, :]).then_inc(x_in, 16)
            for dst, name in LATE:
                sp.dma_start(dst[:], a[name]).then_inc(late_in, 16)
            sp.wait_ge(g_fin, 1)
            for n in range(4):
                sp.dma_start(g_dram[n], graw[:, n, :]).then_inc(row_out, 16)

            def spread(n):
                sp.wait_ge(row_out, 64)
                sp.dma_start(rows[:].rearrange("p b d -> p (b d)"),
                             g_dram[n].rearrange("b d -> (b d)").partition_broadcast(P)).then_inc(row_in, 16)

            spread(0)
            sp.wait_ge(gl_fin, 1)
            sp.dma_start(gate_dram, gs[:]).then_inc(gate_out, 16)
            sp.wait_ge(gate_out, 16)
            sp.dma_start(gateB[:].rearrange("p b h -> p (b h)"),
                         gate_dram.rearrange("b h -> (b h)").partition_broadcast(P)).then_inc(gate_in, 16)
            phase(sp, 1)
            phase(sp, 2)
            for n in range(1, 4):
                spread(n)
                phase(sp, 2 * n + 1)
                if n < 3:
                    phase(sp, 2 * n + 2)
            od = out.rearrange("b (t p) d -> p (b t) d", p=P)
            with sp.Fori(0, NG) as g:
                sp.wait_ge(exp_s[1]["done"], g + 1)
                sp.dma_start(od[:, bass.ts(g, GT), :], x_sb[:, bass.ts(g, GT), :]).then_inc(y_out, 16)
            sp.wait_ge(y_out, 16 * NG)
            phase(sp, 8)

        @block.gpsimd
        def _(pool):
            pool.memset(ident[:], 0.0)
            pool.memset(maskT[:], 0.0)
            pool.memset(maskQ[:], 0.0)
            pool.memset(ones[:], 1.0)
            pool.memset(mhalf[:], -0.5)
            pool.drain()
            pool.affine_select(out=ident[:], in_=ident[:], compare_op=ALU.not_equal, fill=1.0,
                               base=0, pattern=[[-1, P]], channel_multiplier=1)
            pool.affine_select(out=maskT[:], in_=maskT[:], compare_op=ALU.is_ge, fill=NEG,
                               base=0, pattern=[[1, P]], channel_multiplier=-1)
            pool.affine_select(out=maskQ[:], in_=maskQ[:], compare_op=ALU.is_ge, fill=NEG,
                               base=0, pattern=[[-1, P]], channel_multiplier=1)
            pool.drain()
            pool.tensor_copy(ident16[:], ident[:])
            pool.tensor_copy(identb[:], ident[:])
            pool.memset(vs[:], 0.0)
            pool.drain()
            pool.memset(vs[:, :, :, :, DH:DH + 1], 1.0)
            pool.drain().then_inc(idents, 1)

            def keep(n):
                s = norm_s[n]
                pool.wait_ge(s["var"], 1)
                pool.tensor_tensor(rstd[:], rstd[:], mhalf[:, 0:NT], ALU.pow).then_inc(s["rstd"], 1)

                def one(b, par):
                    pool.wait_ge(s["h"], b + 1)
                    pool.tensor_copy(hT[:, bass.ts(b, T)], hcur[:, par, :]).then_inc(s["hT"], 1)

                with pool.Fori(0, B // 2) as i:
                    for par in range(2):
                        one(2 * i + par, par)

            def attention(l):
                s = att_s[l]

                def one(b, first=False):
                    if not first:
                        pool.wait_ge(s["proj"], b)
                    pool.tensor_copy(ha[:], hT[:, bass.ts(b, T)]).then_inc(s["h"], 1)
                    if l == 0:
                        pool.wait_ge(s["n2"], b + 1)
                        pool.tensor_tensor(n2[:, :, 0], n2[:, :, 0], mhalf[:], ALU.pow).then_inc(s["rn"], 1)

                one(0, True)
                with pool.Fori(1, B) as b:
                    one(b)

            def experts(l):
                s = exp_s[l]

                def one(g, par, first=False):
                    if not first:
                        pool.wait_ge(s["done"], g - 1)
                        pool.wait_ge(s["cT"], g - 1)
                    pool.tensor_copy(ccur[l][:, par], comb[l][:, bass.ts(g, GT), :]).then_inc(s["c"], 1)

                one(0, 0, True)
                one(1, 1, True)
                with pool.Fori(1, NG // 2) as i:
                    for par in range(2):
                        one(2 * i + par, par)

            keep(0)
            phase(pool, 1)
            attention(0)
            phase(pool, 2)
            keep(1)
            phase(pool, 3)
            experts(0)
            phase(pool, 4)
            keep(2)
            pool.memset(st[:], 0.0)
            pool.drain()
            pool.memset(st[:, 1, :, 3, 0:1], MSHIFT)
            phase(pool, 5)
            attention(1)
            phase(pool, 6)
            keep(3)
            phase(pool, 7)
            experts(1)
            phase(pool, 8)

        @block.scalar
        def _(act):
            for dst, name in LOADS:
                act.dma_start(dst[:], a[name]).then_inc(w_in, 16)
            act.wait_ge(w_in, 16 * (len(FIRST) + len(LOADS)))
            for l in range(2):
                act.activation(ce[l][:], cT[l][:], ACT.Exp, scale=-1.0).then_inc(silu_e, 1)

            def norm(n):
                s, (l, sh, sc) = norm_s[n], NMOD[n]

                def mod(b, par, first=False):
                    act.wait_ge(s["zT"], b + 1)
                    if not first:
                        act.wait_ge(s["hT"], b - 1)
                        if NX[n]:
                            act.wait_ge(s["x"], b - 1)
                    act.activation(hcur[:, par, :], bank[par][:, 0:T], ACT.Identity,
                                   bias=modT[l][:, sh, bass.ds(b, 1)],
                                   scale=modT[l][:, sc, bass.ds(b, 1)]).then_inc(s["h"], 1)

                def gelu(b, par):
                    act.wait_ge(s["xin"], b + 1)
                    act.activation(xt[:, par, :, 0:HID], xt[:, par, :, 0:HID], ACT.Gelu).then_inc(s["gelu"], 1)

                def one(b, par, first=False, lag=True):
                    mod(b, par, first)
                    if n == 0 and lag:
                        gelu(b - 1, 1 - par)

                one(0, 0, True, False)
                one(1, 1, True)
                with act.Fori(1, B // 2) as i:
                    for par in range(2):
                        one(2 * i + par, par)
                if n == 0:
                    gelu(B - 1, 1)

            act.wait_ge(mod_cp, 2)
            norm(0)
            act.wait_ge(gl_in, 1)
            act.activation(gl[:], gl[:], ACT.Exp, scale=-1.0)
            act.activation(gs[:], gst[:], ACT.Exp, scale=-1.0)
            act.drain().then_inc(gl_exp, 1)
            phase(act, 1)

            def attention(l):
                s = att_s[l]
                W = 512 if l == 0 else 384

                def prep(b, par, first=False):
                    n = 3 if l else 2
                    for i, dst in enumerate([qsT, ksT]):
                        act.wait_ge(s["sT"], n * b + i + 1)
                        act.activation(dst[:, par].rearrange("p j t -> p (j t)"),
                                       M[:, i, :].bitcast(F16), ACT.Copy).then_inc(s["sE"], 1)

                def prep_again(b, par):
                    if l:
                        act.wait_ge(s["sT"], 3 * b + 3)
                        act.activation(qsT[:, par].rearrange("p j t -> p (j t)"),
                                       M[:, 0, :].bitcast(F16), ACT.Copy).then_inc(s["sE"], 1)

                def tail_o(b, first=False):
                    for i in range(2):
                        act.wait_ge(s["pv"], CH * b + 4 * i + 4)
                        act.activation(oT[:].rearrange("p j t -> p (j t)")[:, i * 512:i * 512 + 512],
                                       OP[:, i, :], ACT.Copy).then_inc(s["o"], 1)

                def tail_a(b):
                    act.wait_ge(s["aT"], b + 1)
                    act.activation(aT[:], M[:, 0, 0:T], ACT.Copy).then_inc(s["aE"], 1)

                def exp(b, u, first=False):
                    act.wait_ge(s["score"], CH * b + u + 1)
                    if not (first and u < 4):
                        act.wait_ge(s["pv"], CH * b + u - 3)
                    act.activation(pt[:, u % 4, :, 0:W], SP[u % 2][:, :, 0:W], ACT.Exp,
                                   scale=SCALE).then_inc(s["exp"], 1)

                def one(b, par, first=False, tail=True, nxt=True):
                    if tail:
                        tail_o(b - 1)
                    for u in range(CH):
                        exp(b, u, first)
                        if u == 2 and tail:
                            tail_a(b - 1)
                        if u == 6 and nxt:
                            prep(b + 1, 1 - par)
                    if nxt:
                        prep_again(b + 1, 1 - par)

                prep(0, 0, True)
                prep_again(0, 0)
                one(0, 0, True, tail=False)
                one(1, 1)
                with act.Fori(1, B // 2 - 1) as i:
                    for par in range(2):
                        one(2 * i + par, par)
                one(B - 2, 0)
                one(B - 1, 1, nxt=False)
                tail_o(B - 1)
                tail_a(B - 1)

            def router():
                act.wait_ge(norm_s[1]["rexp"], 1)

            def experts(l, E, F):
                s = exp_s[l]

                def one(g, par, first=False):
                    for e in range(E):
                        for f in range(F):
                            k = e * F + f
                            act.wait_ge(s["hid"], E * F * g + k + 1)
                            if f == 0 and not (first and par == 0 and e < 2):
                                act.wait_ge(s["y"], E * g + e - 1)
                            act.activation(hid[:, e % 2, f, :], bank[k % 4], ACT.Relu,
                                           bias=b1[l][:, k:k + 1]).then_inc(s["relu"], 1)

                one(0, 0, True)
                one(1, 1, True)
                with act.Fori(1, NG // 2) as i:
                    for par in range(2):
                        one(2 * i + par, par)

            attention(0)
            phase(act, 2)
            norm(1)
            act.wait_ge(norm_s[1]["rexp"], 1)
            act.activation(rt[:, :, 0:E0], rt[:, :, 0:E0], ACT.Exp).then_inc(norm_s[1]["gelu"], 1)
            phase(act, 3)
            experts(0, E0, F0)
            phase(act, 4)
            norm(2)
            phase(act, 5)
            attention(1)
            phase(act, 6)
            norm(3)
            act.wait_ge(norm_s[3]["rexp"], 1)
            act.activation(rt[:, :, 0:E1], rt[:, :, 0:E1], ACT.Exp).then_inc(norm_s[3]["gelu"], 1)
            phase(act, 7)
            experts(1, E1, F1)
            phase(act, 8)

        @block.vector
        def _(dve):
            dve.wait_ge(silu_e, 2)
            for l in range(2):
                dve.tensor_scalar(ce[l][:], ce[l][:], 1.0, None, ALU.add)
            dve.drain()
            for l in range(2):
                dve.reciprocal(ce[l][:], ce[l][:])
            dve.drain()
            for l in range(2):
                dve.tensor_tensor(ce[l][:], ce[l][:], cT[l][:], ALU.mult).then_inc(silu_r, 1)
            for l in range(2):
                dve.wait_ge(mod_mm, l + 1)
                dve.tensor_copy(modT[l][:].rearrange("p m b -> p (m b)"), bank[l][:, 0:6 * B])
            dve.drain()
            for l in range(2):
                dve.tensor_scalar(modT[l][:, CA, :], modT[l][:, CA, :], 1.0, None, ALU.add)
                dve.tensor_scalar(modT[l][:, CB, :], modT[l][:, CB, :], 1.0, None, ALU.add).then_inc(mod_cp, 1)
            dve.wait_ge(g_mm, 1)
            dve.tensor_copy(graw.rearrange("p n d -> p (n d)"), bank[2][0:B, :])
            dve.drain()
            flat = [v.rearrange("p n d -> p (n d)") for v in (graw, gsign, gmag)]
            dve.tensor_scalar(flat[1], flat[0], 0.0, 2.0, ALU.is_ge, ALU.mult)
            dve.scalar_tensor_tensor(flat[2], flat[0], -1.0, flat[0], ALU.mult, ALU.max)
            dve.drain()
            dve.tensor_scalar(flat[2], flat[2], 0.25, None, ALU.max)
            dve.drain()
            dve.scalar_tensor_tensor(flat[0], flat[1], -1.0, flat[2], ALU.add, ALU.mult).then_inc(g_fin, 1)
            dve.wait_ge(x_in, 16 * 8)

            def norm(n):
                s = norm_s[n]

                with dve.Fori(0, NT // 8) as i:
                    for k in range(8):
                        dve.bn_stats(stats[:, 8 * i + k, :], x_sb[:, 8 * i + k, :])
                dve.drain()
                dve.tensor_tensor(mean[:], stats[:, :, 1], stats[:, :, 4], ALU.add)
                dve.tensor_tensor(dev[:], stats[:, :, 1], stats[:, :, 4], ALU.subtract)
                dve.tensor_tensor(rstd[:], stats[:, :, 2], stats[:, :, 5], ALU.add)
                dve.drain()
                dve.tensor_scalar(mean[:], mean[:], 0.5, None, ALU.mult)
                dve.tensor_tensor(dev[:], dev[:], dev[:], ALU.mult)
                dve.tensor_scalar(rstd[:], rstd[:], 1.0 / D, LN_EPS, ALU.mult, ALU.add)
                dve.drain()
                dve.scalar_tensor_tensor(rstd[:], dev[:], 0.25, rstd[:], ALU.mult, ALU.add).then_inc(s["var"], 1)
                dve.wait_ge(s["rstd"], 1)

                def ln(b, par, first=False):
                    if not first:
                        dve.wait_ge(s["zT"], b - 1)
                    for t in range(TT):
                        k = bass.ds(2 * b + t, 1)
                        dve.tensor_scalar(z[:, par, t, :], x_sb[:, 2 * b + t, :], mean[:, k],
                                          rstd[:, k], ALU.subtract, ALU.mult).then_inc(s["z"], 1)

                def extra(b, par):
                    if n == 2:
                        return
                    dve.wait_ge(s["x"], b + 1)
                    nx = NX[n]
                    src = bank[2 + par][:, 0:TT * nx].rearrange("p (t x) -> p t x", t=TT)
                    bias = bx[n][:].unsqueeze(1).to_broadcast([P, TT, nx])
                    if n == 3:
                        dve.tensor_tensor(logit[1][:, bass.ts(b, TT), :], src, bias, ALU.add).then_inc(s["xin"], 1)
                        return
                    dve.tensor_tensor(xt[:, par, :, 0:nx], src, bias, ALU.add).then_inc(s["xin"], 1)
                    if n == 0:
                        return
                    dve.drain()
                    dve.tensor_copy(logit[0][:, bass.ts(b, TT), :], xt[:, par, :, 0:E0])
                    for t in range(TT):
                        dve.scalar_tensor_tensor(xt[:, par, t, E0:nx], xt[:, par, t, E0:nx], 0.0, dpw2[:],
                                                 ALU.max, ALU.mult, accum_out=zdp[:, 2 * b + t, :])
                    dve.drain()

                def sums(b, par):
                    if n == 0:
                        dve.wait_ge(s["gmm"], b + 1)
                        dve.tensor_copy(gsum[:, bass.ds(b, 1)], bank[4 + par][0:HID, 0:1]).then_inc(s["gsum"], 1)

                def one(b, par, first=False, lag=1):
                    ln(b, par, first)
                    if lag:
                        extra(b - 1, 1 - par)
                    if lag > 1:
                        sums(b - 2, par)

                one(0, 0, True, 0)
                one(1, 1, True, 1)
                with dve.Fori(1, B // 2) as i:
                    for par in range(2):
                        one(2 * i + par, par, False, 2)
                extra(B - 1, 1)
                sums(B - 2, 0)
                sums(B - 1, 1)

            norm(0)
            dve.wait_ge(gl_mm, 1)
            dve.scalar_tensor_tensor(gl[:], bank[6][0:B, 0:H], 1.0 / T, bg2[:], ALU.mult, ALU.add).then_inc(gl_in, 1)
            dve.wait_ge(gl_exp, 1)
            dve.tensor_scalar(gl[:], gl[:], 1.0, None, ALU.add)
            dve.drain()
            dve.scalar_tensor_tensor(gs[:], gs[:], 1.0, gl[:], ALU.add, ALU.mult)
            dve.drain()
            dve.reciprocal(gs[:], gs[:]).then_inc(gl_fin, 1)
            dve.wait_ge(gate_in, 16)
            dve.wait_ge(row_in, 16)
            phase(dve, 1)

            def attention(l):
                s = att_s[l]

                def prep_qkv(b, par, first=False):
                    dve.wait_ge(s["proj"], b + 1)
                    if not first:
                        dve.wait_ge(s["sT"], (3 if l else 2) * b)
                    for t in range(TT):
                        src = M[:, t, 0:2 * D].rearrange("p (w d) -> p w d", w=2)
                        v = M[:, t, 2 * D:3 * D].rearrange("p (h d) -> p h d", h=H)
                        if l == 0:
                            dve.tensor_tensor(qk[:, :, t, :], src, bqkv[:, 0:2 * D].rearrange("p (w d) -> p w d", w=2),
                                              ALU.add)
                            dve.tensor_tensor(vs[:, par, t, :, 0:DH], v,
                                              bqkv[:, 2 * D:3 * D].rearrange("p (h d) -> p h d", h=H), ALU.add)
                        else:
                            dve.tensor_copy(qk[:, :, t, :], src)
                            dve.tensor_copy(vs[:, par, t, :, 0:DH], v)
                    dve.drain().then_inc(s["qkv"], 1)
                    flat = qk[:].rearrange("p w t d -> p (w t d)")
                    heads = qk[:].rearrange("p w t (h d) -> p (w t h) d", d=DH)
                    if l == 0:
                        dve.tensor_tensor(sq[:].rearrange("p w t d -> p (w t d)"), flat, flat, ALU.mult)
                        dve.drain()
                        dve.tensor_reduce(n2[:], sq[:].rearrange("p w t (h d) -> p (w t h) d", d=DH), AX.X, ALU.add)
                        dve.drain()
                        dve.tensor_scalar(n2[:], n2[:], NORM_EPS ** 2, None, ALU.max).then_inc(s["n2"], 1)
                        dve.wait_ge(s["rn"], b + 1)
                        dve.tensor_tensor(heads, heads, n2[:].to_broadcast([P, 2 * TT * H, DH]), ALU.mult)
                        dve.drain()
                    R = 2 if l == 0 else 1
                    for w in range(2):
                        src = heads[:, w * TT * H:(w + 1) * TT * H, :]
                        hi = st[:, 0, :, 0:3:2, :] if w == 0 else st[:, 1, :, 0:2, :]
                        dve.tensor_copy(hi, src.unsqueeze(2).to_broadcast([P, TT * H, 2, DH]))
                    dve.drain()
                    for w in range(2):
                        src = heads[:, w * TT * H:(w + 1) * TT * H, :]
                        top = st[:, w, :, 0, :]
                        if l == 0:
                            lo = st[:, 0, :, 1:4:2, :] if w == 0 else st[:, 1, :, 2:4, :]
                            ins = dve.tensor_tensor(lo, src.unsqueeze(2).to_broadcast([P, TT * H, 2, DH]),
                                                    top.unsqueeze(2).to_broadcast([P, TT * H, 2, DH]), ALU.subtract)
                        else:
                            lo = st[:, 0, :, 1, :] if w == 0 else st[:, 1, :, 2, :]
                            ins = dve.tensor_tensor(lo, src, top, ALU.subtract)
                        ins.then_inc(s["stack"], 1)

                def prep_max(b):
                    for k in range(12):
                        dve.wait_ge(s["mfill"], 12 * b + k + 1)
                        if k < 8:
                            jj, g = k // 4, k % 4
                            dve.tensor_reduce(mx[:, 1, 2 * jj:2 * jj + 2, g:g + 1],
                                              M[:, k % 2, :].rearrange("p (j k) -> p j k", j=2),
                                              AX.X, ALU.max).then_inc(s["mred"], 1)
                        else:
                            g = k % 4
                            dve.tensor_reduce(mx[:, 0, :, g:g + 1],
                                              M[:, k % 2, :].rearrange("p (j k) -> p j k", j=4),
                                              AX.X, ALU.max).then_inc(s["mred"], 1)
                    dve.drain()
                    dve.tensor_scalar(st[:, 0, :, 3, 0:1], mx[:].rearrange("p t j g -> p (t j g)").unsqueeze(2),
                                      -1.0 / MSHIFT, None, ALU.mult).then_inc(s["mrow"], 1)

                def tail_n(b):
                    dve.wait_ge(s["oT"], 2 * b + 2)
                    for t in range(TT):
                        o = M[:, t, :].rearrange("p (h c) -> p h c", c=32)
                        dve.reciprocal(rs[:, t * H:(t + 1) * H, :], o[:, :, DH:DH + 1])
                    dve.drain()
                    if l == 0:
                        dve.tensor_tensor(rs[:].rearrange("p (t h) o -> p t (h o)", t=TT),
                                          rs[:].rearrange("p (t h) o -> p t (h o)", t=TT),
                                          gateB[:, bass.ds(b, 1), :].to_broadcast([P, TT, H]), ALU.mult)
                        dve.drain()
                    for t in range(TT):
                        o = M[:, t, :].rearrange("p (h c) -> p h c", c=32)
                        dve.tensor_tensor(an[:, t * H:(t + 1) * H, :], o[:, :, 0:DH],
                                          rs[:, t * H:(t + 1) * H, :].to_broadcast([P, H, DH]),
                                          ALU.mult).then_inc(s["an"], 1)

                def tail_x(b):
                    dve.wait_ge(s["wo"], b + 1)
                    w = M[:, 1, 0:TT * D].rearrange("p (t d) -> p t d", t=TT)
                    ga = rows[:, bass.ds(b, 1), :].to_broadcast([P, TT, D])
                    if l == 0:
                        dve.tensor_tensor(ao[:], w, bo[:].unsqueeze(1).to_broadcast([P, TT, D]), ALU.add)
                        dve.drain()
                        dve.tensor_tensor(ao[:], ao[:], ga, ALU.mult)
                    else:
                        dve.tensor_tensor(ao[:], w, ga, ALU.mult)
                    dve.drain()
                    xs = x_sb[:, bass.ts(b, TT), :]
                    dve.tensor_tensor(xs, xs, ao[:], ALU.add).then_inc(s["x"], 1)

                def one(b, par, tail=True, nxt=True):
                    if tail:
                        tail_n(b - 1)
                        tail_x(b - 1)
                    if nxt:
                        prep_qkv(b + 1, 1 - par)
                        if l:
                            prep_max(b + 1)

                prep_qkv(0, 0, True)
                if l:
                    prep_max(0)
                one(0, 0, tail=False)
                one(1, 1)
                with dve.Fori(1, B // 2 - 1) as i:
                    for par in range(2):
                        one(2 * i + par, par)
                one(B - 2, 0)
                one(B - 1, 1, nxt=False)
                tail_n(B - 1)
                tail_x(B - 1)

            def route(n, l, E):
                s = norm_s[n]
                dve.drain()
                if l == 0:
                    for k, (cut, op) in enumerate(K_CUTS):
                        dst = kt if k == 0 else rm
                        dve.tensor_scalar(dst[:], zdp[:], dpb2[:, 0:1], cut, ALU.add, op)
                        dve.drain()
                        if k:
                            dve.tensor_tensor(kt[:], kt[:], rm[:], ALU.add)
                            dve.drain()
                    dve.tensor_scalar(kt[:], kt[:], 1.0, None, ALU.add)
                L = logit[l]
                dve.tensor_reduce(rm[:], L[:], AX.X, ALU.max)
                dve.memset(rank[:, :, 0:E], 0.0)
                dve.drain()
                for o in range(E):
                    other = L[:, :, o:o + 1]
                    if o + 1 < E:
                        dve.tensor_tensor(rt[:, :, o + 1:E], other.to_broadcast([P, NT, E - o - 1]),
                                          L[:, :, o + 1:E], ALU.is_ge)
                    if o:
                        dve.tensor_tensor(rt[:, :, 0:o], other.to_broadcast([P, NT, o]), L[:, :, 0:o], ALU.is_gt)
                    dve.drain()
                    if o + 1 < E:
                        dve.tensor_tensor(rank[:, :, o + 1:E], rank[:, :, o + 1:E], rt[:, :, o + 1:E], ALU.add)
                    if o:
                        dve.tensor_tensor(rank[:, :, 0:o], rank[:, :, 0:o], rt[:, :, 0:o], ALU.add)
                    dve.drain()
                kept = kt[:].to_broadcast([P, NT, E]) if l == 0 else None
                if l == 0:
                    dve.tensor_tensor(rank[:, :, 0:E], rank[:, :, 0:E], kept, ALU.is_lt)
                else:
                    dve.tensor_scalar(rank[:, :, 0:E], rank[:, :, 0:E], 2.0, None, ALU.is_lt)
                dve.tensor_tensor(rt[:, :, 0:E], L[:], rm[:].to_broadcast([P, NT, E]), ALU.subtract)
                dve.drain().then_inc(s["rexp"], 1)
                dve.wait_ge(s["gelu"], 1)
                dve.tensor_tensor(rt[:, :, 0:E], rt[:, :, 0:E], rank[:, :, 0:E], ALU.mult)
                dve.drain()
                dve.tensor_reduce(rm[:], rt[:, :, 0:E], AX.X, ALU.add)
                dve.drain()
                dve.reciprocal(rm[:], rm[:])
                dve.drain()
                dve.tensor_tensor(comb[l][:], rt[:, :, 0:E], rm[:].to_broadcast([P, NT, E]), ALU.mult)

            def experts(l, E, F):
                s = exp_s[l]

                def one(g, par):
                    dve.wait_ge(s["cT"], g + 1)
                    dve.tensor_copy(cTr[l][:], bank[7][0:E, :]).then_inc(s["cE"], 1)
                    dve.wait_ge(s["b2"], g + 1)
                    dve.tensor_copy(acc[:].rearrange("p t d -> p (t d)"), bank[6])
                    dve.drain()
                    for e in range(E):
                        dve.wait_ge(s["y"], E * g + e + 1)
                        for t in range(GT):
                            dve.scalar_tensor_tensor(acc[:, t, :], bank[4 + e % 2][:, t * D:(t + 1) * D],
                                                     ccur[l][:, par, t, e:e + 1], acc[:, t, :], ALU.mult, ALU.add)
                        dve.drain().then_inc(s["acc"], 1)
                    for k in range(2):
                        v = acc[:, 2 * k:2 * k + 2, :]
                        dve.tensor_tensor(v, v, rows[:, bass.ds(2 * g + k, 1), :].to_broadcast([P, TT, D]), ALU.mult)
                    dve.drain()
                    xs = x_sb[:, bass.ts(g, GT), :]
                    dve.tensor_tensor(xs, xs, acc[:], ALU.add).then_inc(s["done"], 1)

                with dve.Fori(0, NG // 2) as i:
                    for par in range(2):
                        one(2 * i + par, par)

            attention(0)
            phase(dve, 2)
            norm(1)
            route(1, 0, E0)
            dve.wait_ge(row_in, 32)
            phase(dve, 3)
            experts(0, E0, F0)
            phase(dve, 4)
            norm(2)
            dve.wait_ge(row_in, 48)
            phase(dve, 5)
            attention(1)
            phase(dve, 6)
            norm(3)
            route(3, 1, E1)
            dve.wait_ge(row_in, 64)
            phase(dve, 7)
            experts(1, E1, F1)
            phase(dve, 8)

        @block.tensor
        def _(pe):
            pe.wait_ge(idents, 1)
            pe.wait_ge(w_in, 16 * (len(FIRST) + len(LOADS)))
            for l in range(2):
                pe.wait_ge(silu_r, l + 1)
                for m in range(6):
                    last = pe.matmul(bank[l][:, m * B:(m + 1) * B], wmod[l][:, m * D:(m + 1) * D], ce[l][:],
                                     start=True, stop=True)
                last.then_inc(mod_mm, 1)
            for n in range(4):
                l, m = n // 2, (GA, GB)[n % 2]
                last = pe.matmul(bank[2][0:B, n * D:(n + 1) * D], ce[l][:], wmod[l][:, m * D:(m + 1) * D],
                                 start=True, stop=True)
            last.then_inc(g_mm, 1)
            pe.wait_ge(mod_cp, 2)
            pe.wait_ge(g_fin, 1)

            def norm(n):
                s = norm_s[n]

                def turn(b, par, first=False):
                    if not first:
                        pe.wait_ge(s["h"], b - 1)
                    for t in range(TT):
                        pe.wait_ge(s["z"], TT * b + t + 1)
                        last = pe.transpose(bank[par][:, t * P:(t + 1) * P], z[:, par, t, :], ident[:])
                    last.then_inc(s["zT"], 1)

                def project(b, par, first=False):
                    if not NX[n]:
                        return
                    pe.wait_ge(s["h"], b + 1)
                    if not first:
                        pe.wait_ge(s["xin"], b - 1)
                    for t in range(TT):
                        last = pe.matmul(bank[2 + par][:, t * NX[n]:(t + 1) * NX[n]],
                                         hcur[:, par, t * P:(t + 1) * P], wx[n][:], start=True, stop=True)
                    last.then_inc(s["x"], 1)

                def gate_sum(b, par, first=False):
                    if n:
                        return
                    pe.wait_ge(s["gelu"], b + 1)
                    if not first:
                        pe.wait_ge(s["gsum"], b - 1)
                    for t in range(TT):
                        last = pe.matmul(bank[4 + par][0:HID, 0:1], xt[:, par, t, 0:HID], ones[:],
                                         start=(t == 0), stop=(t == TT - 1))
                    last.then_inc(s["gmm"], 1)

                turn(0, 0, True)
                turn(1, 1, True)
                project(0, 0, True)
                turn(2, 0)
                project(1, 1, True)
                gate_sum(0, 0, True)
                turn(3, 1)
                project(2, 0)
                gate_sum(1, 1, True)
                with pe.Fori(2, B // 2) as i:
                    for par in range(2):
                        turn(2 * i + par, par)
                        project(2 * i + par - 1, 1 - par)
                        gate_sum(2 * i + par - 2, par)
                project(B - 1, 1)
                gate_sum(B - 2, 0)
                gate_sum(B - 1, 1)

            norm(0)
            pe.wait_ge(norm_s[0]["gsum"], B)
            pe.matmul(bank[6][0:B, 0:H], gsum[:], wg2[:], start=True, stop=True).then_inc(gl_mm, 1)
            phase(pe, 1)

            def attention(l):
                s = att_s[l]
                per = 3 if l else 2

                def prep_proj(b, first=False):
                    pe.wait_ge(s["h"], b + 1)
                    if not first:
                        pe.wait_ge(s["x"], b - 1)
                        pe.wait_ge(s["aE"], b - 1)
                    for t in range(TT):
                        last = pe.matmul(M[:, t, 0:3 * D], ha[:, t * P:(t + 1) * P], wqkv[l][:], start=True, stop=True)
                    last.then_inc(s["proj"], 1)

                def turn_stack(b, w, bankno):
                    to = M[:, bankno, :].bitcast(F16)
                    for j in range(NJ):
                        for t in range(TT):
                            src = st[:, w, t * H + j * HG:t * H + (j + 1) * HG].rearrange("p h r d -> p (h r d)")
                            last = pe.transpose(to[:, j * T + t * P:j * T + (t + 1) * P], src, ident16[:])
                    last.then_inc(s["sT"], 1)

                def prep_turn(b):
                    pe.wait_ge(s["qkv"], b + 1)
                    for w in range(2):
                        pe.wait_ge(s["stack"], 2 * b + w + 1)
                        turn_stack(b, w, w)

                def prep_max(b, par, k):
                    if k == 0:
                        pe.wait_ge(s["sE"], per * b + 2)
                    if k >= 2:
                        pe.wait_ge(s["mred"], 12 * b + k - 1)
                    to, g = M[:, k % 2, :], k % 4
                    if k < 8:
                        v = to.rearrange("p (j k) -> p j k", j=2)
                        pe.matmul(v[:, :, P:T], identb[:], maskQ[:].unsqueeze(1).to_broadcast([P, 2, P]),
                                  start=True, stop=False, skip_group_check=True)
                        js, q0, kn = (2 * (k // 4), 2 * (k // 4) + 1), P, T
                    else:
                        v = to.rearrange("p (j k) -> p j k", j=4)
                        pe.matmul(v[:, :, :], identb[:], maskQ[:].unsqueeze(1).to_broadcast([P, 4, P]),
                                  start=True, stop=False, skip_group_check=True)
                        js, q0, kn = range(4), 0, P
                    for n, j in enumerate(js):
                        last = pe.matmul(v[:, n, :], qsT[32 * g:32 * g + 3 * DH, par, j, q0:q0 + P],
                                         ksT[32 * g:32 * g + 3 * DH, par, j, 0:kn], start=False, stop=True,
                                         skip_group_check=True, tile_position=(32 * g, 0))
                    last.then_inc(s["mfill"], 1)

                def prep_requeue(b):
                    pe.wait_ge(s["mrow"], b + 1)
                    turn_stack(b, 0, 0)

                def score(b, par, u, first=False):
                    if u == 0:
                        pe.wait_ge(s["sE"], per * b + per)
                    if not (first and u < 2):
                        pe.wait_ge(s["exp"], CH * b + u - 1)
                    j = u // 2
                    for i in range(2):
                        g = 2 * (u % 2) + i
                        to = SP[u % 2][:, i, :]
                        if l:
                            diag = to[:, 0:512].rearrange("p (k q) -> p k q", k=2)[:, :, 0:P]
                            pe.matmul(diag, identb[:], maskT[:].unsqueeze(1).to_broadcast([P, 2, P]),
                                      start=True, stop=False, skip_group_check=True)
                    for i in range(2):
                        g = 2 * (u % 2) + i
                        to = SP[u % 2][:, i, :]
                        for k in range(TT):
                            q0 = P if (l and k) else 0
                            last = pe.matmul(to[:, k * T:k * T + T - q0],
                                             ksT[32 * g:32 * g + 32, par, j, k * P:(k + 1) * P],
                                             qsT[32 * g:32 * g + 32, par, j, q0:T], start=(l == 0), stop=True,
                                             skip_group_check=True, tile_position=(32 * g, 0))
                    last.then_inc(s["score"], 1)

                def values(b, par, u, first=False):
                    pe.wait_ge(s["exp"], CH * b + u + 1)
                    if not first and u % 4 == 0:
                        pe.wait_ge(s["o"], 2 * b + u // 4 - 1)
                    j = u // 2
                    for k in range(TT):
                        q0 = P if (l and k) else 0
                        for i in range(2):
                            g = 2 * (u % 2) + i
                            c = (j % 2) * T
                            last = pe.matmul(OP[32 * g:32 * g + 32, j // 2, c + q0:c + T],
                                             vs[:, par, k, HG * j + g, :],
                                             pt[:, u % 4, i, k * T:k * T + T - q0],
                                             start=(k == 0), stop=(k == TT - 1),
                                             skip_group_check=True, tile_position=(0, 32 * g))
                    last.then_inc(s["pv"], 1)

                def tail_turn(b):
                    pe.wait_ge(s["o"], 2 * b + 2)
                    for t in range(TT):
                        for j in range(NJ):
                            last = pe.transpose(M[:, t, j * P:(j + 1) * P], oT[:, j, t * P:(t + 1) * P], ident[:])
                        last.then_inc(s["oT"], 1)

                def tail_an(b):
                    pe.wait_ge(s["an"], 2 * b + 2)
                    for t in range(TT):
                        last = pe.transpose(M[:, 0, t * P:(t + 1) * P],
                                            an[:, t * H:(t + 1) * H, :].rearrange("p h d -> p (h d)"), ident[:])
                    last.then_inc(s["aT"], 1)

                def tail_wo(b):
                    pe.wait_ge(s["aE"], b + 1)
                    for t in range(TT):
                        last = pe.matmul(M[:, 1, t * D:(t + 1) * D], aT[:, t * P:(t + 1) * P], wo[l][:],
                                         start=True, stop=True)
                    last.then_inc(s["wo"], 1)

                def one(b, par, first=False, tail=True, nxt=True):
                    for u in range(CH):
                        score(b, par, u, first)
                        if u:
                            values(b, par, u - 1, first)
                        if tail and u == 0:
                            tail_turn(b - 1)
                        if tail and u == 1:
                            tail_an(b - 1)
                        if tail and u == 3:
                            tail_wo(b - 1)
                        if nxt and u == 4:
                            prep_proj(b + 1, first)
                        if nxt and u == 6:
                            prep_turn(b + 1)
                    values(b, par, CH - 1, first)
                    if nxt and l:
                        for k in range(12):
                            prep_max(b + 1, 1 - par, k)
                        prep_requeue(b + 1)

                prep_proj(0, True)
                prep_turn(0)
                if l:
                    for k in range(12):
                        prep_max(0, 0, k)
                    prep_requeue(0)
                one(0, 0, True, tail=False)
                one(1, 1)
                with pe.Fori(1, B // 2 - 1) as i:
                    for par in range(2):
                        one(2 * i + par, par)
                one(B - 2, 0)
                one(B - 1, 1, nxt=False)
                pe.wait_ge(s["x"], B - 1)
                tail_turn(B - 1)
                tail_an(B - 1)
                tail_wo(B - 1)

            def experts(l, E, F):
                s = exp_s[l]
                N = GT * P

                def weights(g, par):
                    pe.wait_ge(s["c"], g + 1)
                    for t in range(GT):
                        last = pe.transpose(bank[7][0:E, t * P:(t + 1) * P], ccur[l][:, par, t, :], ident[:])
                    last.then_inc(s["cT"], 1)

                def bias2(g, first):
                    pe.wait_ge(s["cE"], g + 1)
                    if not first:
                        pe.wait_ge(s["acc"], E * g)
                    for t in range(GT):
                        last = pe.matmul(bank[6][:, t * D:(t + 1) * D], cTr[l][:, t * P:(t + 1) * P], b2[l][:],
                                         start=True, stop=True)
                    last.then_inc(s["b2"], 1)

                def hidden(g, e, first):
                    for f in range(F):
                        k = e * F + f
                        if not (first and k < 4):
                            pe.wait_ge(s["relu"], E * F * g + k - 3)
                        pe.matmul(bank[k % 4], w1[l][:, e, f * P:(f + 1) * P], hT[:, bass.ts(g, N)],
                                  start=True, stop=True).then_inc(s["hid"], 1)

                def outputs(g, e, first):
                    pe.wait_ge(s["relu"], E * F * g + (e + 1) * F)
                    if not (first and e < 2):
                        pe.wait_ge(s["acc"], E * g + e - 1)
                    for t in range(GT):
                        for f in range(F):
                            last = pe.matmul(bank[4 + e % 2][:, t * D:(t + 1) * D],
                                             hid[:, e % 2, f, t * P:(t + 1) * P], w2[l][:, e * F + f, :],
                                             start=(f == 0), stop=(f == F - 1))
                    last.then_inc(s["y"], 1)

                def one(g, par, first=False):
                    weights(g, par)
                    for e in range(E):
                        hidden(g, e, first)
                        if e == 0:
                            bias2(g, first)
                        else:
                            outputs(g, e - 1, first)
                    outputs(g, E - 1, first)

                one(0, 0, True)
                one(1, 1)
                with pe.Fori(1, NG // 2) as i:
                    for par in range(2):
                        one(2 * i + par, par)

            attention(0)
            phase(pe, 2)
            norm(1)
            phase(pe, 3)
            pe.wait_ge(late_in, 16 * len(LATE))
            experts(0, E0, F0)
            phase(pe, 4)
            norm(2)
            phase(pe, 5)
            attention(1)
            phase(pe, 6)
            norm(3)
            phase(pe, 7)
            experts(1, E1, F1)
            phase(pe, 8)


def layout(i):
    import numpy as np

    def c(v):
        return np.ascontiguousarray(v)

    def rep(v, n=P):
        return c(np.broadcast_to(np.asarray(v).reshape(1, -1), (n, np.asarray(v).size)))

    def experts(w, b, w2, b2, e, f):
        return (c(np.transpose(w, (1, 0, 2))),
                c(np.transpose(np.asarray(w2).reshape(e * f, P, D), (1, 0, 2))),
                c(np.asarray(b).reshape(e * f, P).T), c(b2))

    i = {k: np.asarray(v) for k, v in i.items()}
    a = {"x": c(i["L0_attn_x"])}
    for l in range(2):
        a[f"cT{l}"] = c(i[f"L{l}_c"].T)
        a[f"wmod{l}"] = c(i[f"L{l}_wmod"])
    a["wqkv0"] = c(np.concatenate([i["L0_attn_Wq"].T, i["L0_attn_Wk"].T, i["L0_attn_Wv"].T], axis=1))
    a["wqkv1"] = c(np.concatenate([i["L1_attn_Wq"], i["L1_attn_Wkv"]], axis=1))
    a["wo0"], a["wo1"] = c(i["L0_attn_Wo"].T), c(i["L1_attn_Wo"])
    a["bqkv0"] = rep(np.concatenate([i["L0_attn_bq"], i["L0_attn_bk"], i["L0_attn_bv"]]))
    a["bo0"] = rep(i["L0_attn_bo"])
    a["wx0"], a["bx0"] = c(i["L0_attn_Wg1"].T), rep(i["L0_attn_bg1"])
    a["wx1"] = c(np.concatenate([i["L0_ffn_gate_w"], i["L0_ffn_dp_w1"]], axis=1))
    a["bx1"] = rep(np.concatenate([i["L0_ffn_gate_b"], i["L0_ffn_dp_b1"]]))
    a["wx3"], a["bx3"] = c(i["L1_ffn_Wg"]), rep(i["L1_ffn_bg"])
    a["dpw2"], a["dpb2"] = rep(i["L0_ffn_dp_w2"]), rep(i["L0_ffn_dp_b2"])
    a["wg2"], a["bg2"], a["g"] = c(i["L0_attn_Wg2"].T), rep(i["L0_attn_bg2"], B), rep(i["L0_attn_g"], B)
    a["w1_0"], a["w2_0"], a["b1_0"], a["b2_0"] = experts(
        i["L0_ffn_ew1"], i["L0_ffn_eb1"], i["L0_ffn_ew2"], i["L0_ffn_eb2"], E0, F0)
    a["w1_1"], a["w2_1"], a["b1_1"], a["b2_1"] = experts(
        i["L1_ffn_W1"], i["L1_ffn_b1"], i["L1_ffn_W2"], i["L1_ffn_b2"], E1, F1)
    return a


def kernel(**inputs):
    import concourse.bacc as bacc
    from concourse.bass_utils import run_bass_kernel_spmd

    nc = bacc.Bacc("TRN2", target_bir_lowering=False, num_devices=1)
    arrays = layout(inputs)
    aps = {n: nc.dram_tensor(f"in_{n}", v.shape, F32, kind="ExternalInput").ap() for n, v in arrays.items()}
    out = nc.dram_tensor("out", (B, T, D), F32, kind="ExternalOutput").ap()
    program(nc, aps, out)
    r = run_bass_kernel_spmd(nc, [{f"in_{n}": v for n, v in arrays.items()}], core_ids=[0])
    return r.results[0]["out"]
```

```python
from contextlib import ExitStack

import concourse.bass as bass
from concourse import mybir

F32 = mybir.dt.float32
F16 = mybir.dt.float16
BF16 = mybir.dt.bfloat16
I32 = mybir.dt.int32
ALU = mybir.AluOpType
ACT = mybir.ActivationFunctionType
AX = mybir.AxisListType

B, T, D = 32, 256, 128
P = 128
TT = T // P
NT = B * TT
H, DH = 16, 8
HG = 4
NJ = H // HG
HID = 64
E0, F0 = 4, 2
E1, F1 = 8, 4
GT = 4
NG = NT // GT
LN_EPS = 1e-5
NORM_EPS = 1e-12
SCALE = DH ** -0.5
NEG = -1e30
MSHIFT = 256.0
CH = 8

import math
K_CUTS = [(math.log(math.exp(0.5 + 1.5 * (c - 1.0) / 3.0) - 1.0), op)
          for c, op in ((1.5, ALU.is_ge), (2.5, ALU.is_gt), (3.5, ALU.is_ge))]

SA, CA, GA, SB, CB, GB = range(6)
NX = [HID, E0 + HID, 0, E1]
NMOD = [(0, SA, CA), (0, SB, CB), (1, SA, CA), (1, SB, CB)]


def program(nc, a, out):
    ctx = ExitStack()
    with ctx:
        def sb(name, shape, dt=F32):
            return ctx.enter_context(nc.sbuf_tensor(name, shape, dt))

        def pb(name, shape, dt=F32):
            return ctx.enter_context(nc.psum_tensor(name, shape, dt))

        def sem(name):
            return ctx.enter_context(nc.semaphore(name))

        x_sb = sb("x_sb", [P, NT, D])
        hT = sb("hT", [P, NT * P])
        rows = sb("rows", [P, B, D])
        modT = [sb(f"modT{l}", [P, 6, B]) for l in range(2)]
        wqkv = [sb(f"wqkv{l}", [P, 3 * D]) for l in range(2)]
        wo = [sb(f"wo{l}", [P, D]) for l in range(2)]
        bqkv = sb("bqkv", [P, 3 * D])
        bo = sb("bo", [P, D])
        wx = [sb("wx0", [P, NX[0]]), sb("wx1", [P, NX[1]]), None, sb("wx3", [P, NX[3]])]
        bx = [sb("bx0", [P, NX[0]]), sb("bx1", [P, NX[1]]), None, sb("bx3", [P, NX[3]])]
        dpw2 = sb("dpw2", [P, HID])
        dpb2 = sb("dpb2", [P, 1])
        wg2 = sb("wg2", [HID, H])
        bg2 = sb("bg2", [B, H])
        gst = sb("gst", [B, H])
        shared = sb("shared", [P, 2 * E1 * F1 * P])
        half = E1 * F1 * P
        w1 = [sb("w1_0", [P, E0, F0 * P]), shared[:, 0:half].rearrange("p (e f) -> p e f", e=E1)]
        w2 = [sb("w2_0", [P, E0 * F0, D]), shared[:, half:2 * half].rearrange("p (e d) -> p e d", d=D)]
        b1 = [sb("b1_0", [P, E0 * F0]), sb("b1_1", [P, E1 * F1])]
        b2 = [sb("b2_0", [E0, D]), sb("b2_1", [E1, D])]
        logit = [sb("logit0", [P, NT, E0]), sb("logit1", [P, NT, E1])]
        comb = [sb("comb0", [P, NT, E0]), sb("comb1", [P, NT, E1])]
        zdp = sb("zdp", [P, NT, 1])
        gsum = sb("gsum", [HID, B])
        gateB = sb("gateB", [P, B, H])
        ident = sb("ident", [P, P])
        ident16 = sb("ident16", [P, P], F16)
        identb = sb("identb", [P, P], BF16)
        ones = sb("ones", [P, 1])
        spare = sb("spare", [P, CH])
        maskT = sb("maskT", [P, P], BF16)
        maskQ = sb("maskQ", [P, P], BF16)
        cT = [sb(f"cT{l}", [P, B]) for l in range(2)]
        ce = [sb(f"ce{l}", [P, B]) for l in range(2)]
        pt = sb("pt", [P, 4, 2, 512])
        free = pt[:].rearrange("p a b c -> p (a b c)")
        wmod = [free[:, l * 6 * D:(l + 1) * 6 * D] for l in range(2)]
        graw, gsign, gmag = [free[0:B, 12 * D + n * 4 * D:12 * D + (n + 1) * 4 * D].rearrange(
            "p (n d) -> p n d", n=4) for n in range(3)]
        gl = sb("gl", [B, H])
        gs = sb("gs", [B, H])
        stats = sb("stats", [P, NT, 6])
        mean = sb("mean", [P, NT])
        rstd = sb("rstd", [P, NT])
        dev = sb("dev", [P, NT])
        var = sb("var", [P, NT])
        z = sb("z", [P, 2, TT, D])
        hcur = sb("hcur", [P, 2, T])
        xt = sb("xt", [P, 2, TT, HID + E0])
        rt = sb("rt", [P, NT, E1])
        rank = sb("rank", [P, NT, E1])
        rm = sb("rm", [P, NT, 1])
        kt = sb("kt", [P, NT, 1])
        ha = sb("ha", [P, T])
        qkv = sb("qkv", [P, 3, TT, D])
        qk = qkv[:, 0:2]
        sq = sb("sq", [P, 2, TT, D])
        n2 = sb("n2", [P, 2 * TT * H, 1])
        rn = sb("rn", [P, 2 * TT * H, 1])
        nt = sb("nt", [P, 2 * TT * H, 1])
        st = sb("st", [P, 2, TT * H, 4, DH], F16)
        qsT = sb("qsT", [P, NJ, T], F16)
        qz = shared[:, 0:HG * NJ * T].bitcast(F16).rearrange("p (b g j t) -> p b g j t", b=2, g=HG, j=NJ)
        ksT = sb("ksT", [P, 2, NJ, T], F16)
        vs = sb("vs", [P, 2, TT, H, 32])
        oT = sb("oT", [P, NJ, T])
        rs = sb("rs", [P, TT * H, 1])
        an = sb("an", [P, TT * H, DH])
        aT = sb("aT", [P, T])
        ao = sb("ao", [P, TT, D])
        mx = sb("mx", [P, TT, NJ, HG])
        hid = pt[:].rearrange("p (e a) b n -> p e (a b) n", e=2)
        ccur = [sb("ccur0", [P, 2, GT, E0]), sb("ccur1", [P, 2, GT, E1])]
        cTr = [sb("cTr0", [E0, GT * P]), sb("cTr1", [E1, GT * P])]
        acc = sq[:].rearrange("p w t d -> p (w t) d")

        SP = [pb("SP0", [P, 2, 512]), pb("SP1", [P, 2, 512])]
        OP = pb("OP", [P, 2, 512])
        M = pb("M", [P, 2, 512])
        bank = [SP[0][:, 0, :], SP[0][:, 1, :], SP[1][:, 0, :], SP[1][:, 1, :],
                OP[:, 0, :], OP[:, 1, :], M[:, 0, :], M[:, 1, :]]

        g_dram = [nc.dram_tensor(f"g_dram{n}", (B, D), F32, kind="Internal").ap() for n in range(4)]
        gate_dram = nc.dram_tensor("gate_dram", (B, H), F32, kind="Internal").ap()

        phase_end = sem("phase_end")
        w_in, late_in = sem("w_in"), sem("late_in")
        x_in = [sem(f"x_in{i}") for i in range(8)]
        row_out, row_in, gate_out, gate_in = sem("row_out"), sem("row_in"), sem("gate_out"), sem("gate_in")
        y_out = sem("y_out")
        masks = sem("masks")
        idents = sem("idents")
        silu_e, silu_r = sem("silu_e"), sem("silu_r")
        mod_mm, mod_cp, g_mm, g_fin = sem("mod_mm"), sem("mod_cp"), sem("g_mm"), sem("g_fin")
        gl_mm, gl_in, gl_exp, gl_fin = sem("gl_mm"), sem("gl_in"), sem("gl_exp"), sem("gl_fin")

        def sems(kind, n, names):
            return {k: sem(f"{kind}{n}_{k}") for k in names.split()}

        norm_s = [sems("norm", n, "z zT h hT x xin gelu gmm gsum rexp") for n in range(4)]
        att_s = [sems("att", l, "h proj sel qkv stack sT sE mfill mred mrow score exp pv o oT an aT aE wo wr x qz guess rn vs")
                 for l in range(2)]
        exp_s = [sems("exp", l, "c cT cE hid relu y b2 acc done") for l in range(2)]

        block = ctx.enter_context(nc.Block())
        ENGINES = 5

        def phase(eng, n):
            eng.drain().then_inc(phase_end, 1)
            eng.wait_ge(phase_end, ENGINES * n)

        LOADS = [(wqkv[0], "wqkv0"), (wqkv[1], "wqkv1"), (wo[0], "wo0"), (wo[1], "wo1"),
                 (bqkv, "bqkv0"), (bo, "bo0"), (wx[0], "wx0"), (wx[1], "wx1"), (wx[3], "wx3"),
                 (bx[0], "bx0"), (bx[1], "bx1"), (bx[3], "bx3"), (dpw2, "dpw2"), (dpb2, "dpb2"),
                 (wg2, "wg2"), (bg2, "bg2"), (gst, "g"), (b1[0], "b1_0"), (b1[1], "b1_1"),
                 (b2[0], "b2_0"), (b2[1], "b2_1")]
        FIRST = [(cT[0], "cT0"), (cT[1], "cT1"), (wmod[0], "wmod0"), (wmod[1], "wmod1")]
        LATE = [(w1[0], "w1_0"), (w2[0], "w2_0")]
        LAST = [(w1[1], "w1_1"), (w2[1], "w2_1")]

        @block.sync
        def _(sp):
            for dst, name in FIRST:
                sp.dma_start(dst[:, :], a[name]).then_inc(w_in, 16)
            xd = a["x"].rearrange("b (t p) d -> p (b t) d", p=P)
            for i in range(8):
                sp.dma_start(x_sb[:, i * 8:i * 8 + 8, :], xd[:, i * 8:i * 8 + 8, :]).then_inc(x_in[i], 16)
            for dst, name in LATE:
                sp.dma_start(dst[:], a[name]).then_inc(late_in, 16)
            sp.wait_ge(g_fin, 1)
            for n in range(4):
                sp.dma_start(g_dram[n], graw[:, n, :]).then_inc(row_out, 16)

            def spread(n):
                sp.wait_ge(row_out, 64)
                sp.dma_start(rows[:].rearrange("p b d -> p (b d)"),
                             g_dram[n].rearrange("b d -> (b d)").partition_broadcast(P)).then_inc(row_in, 16)

            spread(0)
            sp.wait_ge(gl_fin, 1)
            sp.dma_start(gate_dram, gs[:]).then_inc(gate_out, 16)
            sp.wait_ge(gate_out, 16)
            sp.dma_start(gateB[:].rearrange("p b h -> p (b h)"),
                         gate_dram.rearrange("b h -> (b h)").partition_broadcast(P)).then_inc(gate_in, 16)
            phase(sp, 1)
            phase(sp, 2)
            for n in range(1, 4):
                if n == 3:
                    for dst, name in LAST:
                        sp.dma_start(dst, a[name]).then_inc(late_in, 16)
                spread(n)
                phase(sp, 2 * n + 1)
                if n < 3:
                    phase(sp, 2 * n + 2)
            od = out.rearrange("b (t p) d -> p (b t) d", p=P)
            with sp.Fori(0, NG) as g:
                sp.wait_ge(exp_s[1]["done"], g + 1)
                sp.dma_start(od[:, bass.ts(g, GT), :], x_sb[:, bass.ts(g, GT), :]).then_inc(y_out, 16)
            sp.wait_ge(y_out, 16 * NG)
            phase(sp, 8)

        @block.gpsimd
        def _(pool):
            one_s = ones[:, 0:1].to_broadcast([P, T])
            pool.memset(ident[:], 0.0)
            pool.memset(maskT[:], 0.0)
            pool.memset(maskQ[:], 0.0)
            pool.memset(ones[:], 1.0)
            pool.drain()
            pool.affine_select(out=ident[:], in_=ident[:], compare_op=ALU.not_equal, fill=1.0,
                               base=0, pattern=[[-1, P]], channel_multiplier=1)
            pool.affine_select(out=maskT[:], in_=maskT[:], compare_op=ALU.is_ge, fill=NEG,
                               base=0, pattern=[[1, P]], channel_multiplier=-1)
            pool.affine_select(out=maskQ[:], in_=maskQ[:], compare_op=ALU.is_ge, fill=NEG,
                               base=0, pattern=[[-1, P]], channel_multiplier=1)
            pool.drain()
            pool.tensor_copy(ident16[:], ident[:])
            pool.tensor_copy(identb[:], ident[:])
            pool.memset(vs[:], 0.0)
            pool.memset(shared[:, 0:HG * NJ * T], 0.0)
            pool.drain()
            pool.memset(vs[:, :, :, :, DH:DH + 1], 1.0)
            pool.drain().then_inc(idents, 1)

            def keep(n):
                s = norm_s[n]

                def one(b, par):
                    pool.wait_ge(s["h"], b + 1)
                    pool.tensor_tensor(hT[:, bass.ts(b, T)], hcur[:, par, :], one_s[:, 0:T],
                                       ALU.mult).then_inc(s["hT"], 1)

                with pool.Fori(0, B // 2) as i:
                    for par in range(2):
                        one(2 * i + par, par)

            def attention(l):
                s = att_s[l]

                def fetch(b, first=False):
                    if not first:
                        pool.wait_ge(s["proj"], 2 * b)
                    pool.tensor_tensor(ha[:], hT[:, bass.ts(b, T)], one_s[:, 0:T], ALU.mult).then_inc(s["h"], 1)

                def newton(b):
                    pool.wait_ge(s["guess"], b + 1)
                    for k in range(3):
                        pool.tensor_tensor(nt[:], rn[:], rn[:], ALU.mult)
                        pool.drain()
                        pool.tensor_tensor(nt[:], nt[:], n2[:], ALU.mult)
                        pool.drain()
                        pool.tensor_scalar(nt[:], nt[:], -0.5, 1.5, ALU.mult, ALU.add)
                        pool.drain()
                        last = pool.tensor_tensor(rn[:], rn[:], nt[:], ALU.mult)
                        if k < 2:
                            pool.drain()
                    last.then_inc(s["rn"], 1)

                def place_v(b, par, first=False):
                    pool.wait_ge(s["qkv"], b + 1)
                    if not first:
                        pool.wait_ge(s["pv"], CH * (b - 1))
                    v = qkv[:, 2].rearrange("p t (h d) -> p (t h) d", d=DH)
                    pool.tensor_tensor(vs[:, par, :, :, 0:DH].rearrange("p t h d -> p (t h) d"), v, one_s[:, 0:T].rearrange("p (n d) -> p n d", d=DH),
                                       ALU.mult).then_inc(s["vs"], 1)

                def select(b, u):
                    pool.wait_ge(s["exp"], CH * b + u + 1)
                    pool.tensor_tensor(spare[:, u:u + 1], ones[:], ones[:], ALU.mult)
                    for i in range(2):
                        diag = pt[:, u % 4, i, :].rearrange("p (k q) -> p k q", k=2)[:, :, 0:P]
                        last = pool.affine_select(out=diag, in_=diag, compare_op=ALU.is_ge, fill=0.0, base=0,
                                                  pattern=[[0, 2], [1, P]], channel_multiplier=-1)
                    last.then_inc(s["sel"], 1)

                def one(b, par, first=False, ahead=3):
                    if l:
                        pool.drain()
                        select(b, 0)
                    if ahead >= 1:
                        place_v(b + 1, 1 - par, first)
                    if l:
                        for u in range(1, CH):
                            select(b, u)
                    if ahead >= 3:
                        fetch(b + 3)
                    if l == 0 and ahead >= 2:
                        newton(b + 2)

                fetch(0, True)
                fetch(1)
                if l == 0:
                    newton(0)
                place_v(0, 0, True)
                fetch(2)
                if l == 0:
                    newton(1)
                one(0, 0, True)
                one(1, 1)
                with pool.Fori(1, B // 2 - 2) as i:
                    for par in range(2):
                        one(2 * i + par, par)
                one(B - 4, 0)
                one(B - 3, 1, ahead=2)
                one(B - 2, 0, ahead=1)
                one(B - 1, 1, ahead=0)

            def experts(l):
                s = exp_s[l]

                def one(g, par, first=False):
                    if not first:
                        pool.wait_ge(s["done"], g - 1)
                        pool.wait_ge(s["cT"], g - 1)
                    pool.tensor_copy(ccur[l][:, par], comb[l][:, bass.ts(g, GT), :]).then_inc(s["c"], 1)

                one(0, 0, True)
                one(1, 1, True)
                with pool.Fori(1, NG // 2) as i:
                    for par in range(2):
                        one(2 * i + par, par)

            keep(0)
            phase(pool, 1)
            attention(0)
            phase(pool, 2)
            keep(1)
            phase(pool, 3)
            experts(0)
            phase(pool, 4)
            keep(2)
            pool.memset(st[:], 0.0)
            pool.drain()
            pool.memset(st[:, 1, :, 3, 0:1], MSHIFT)
            phase(pool, 5)
            attention(1)
            phase(pool, 6)
            keep(3)
            phase(pool, 7)
            experts(1)
            phase(pool, 8)

        @block.scalar
        def _(act):
            for dst, name in LOADS:
                act.dma_start(dst[:], a[name]).then_inc(w_in, 16)
            act.wait_ge(w_in, 16 * (len(FIRST) + len(LOADS)))
            for l in range(2):
                act.activation(ce[l][:], cT[l][:], ACT.Exp, scale=-1.0).then_inc(silu_e, 1)

            def norm(n):
                s, (l, sh, sc) = norm_s[n], NMOD[n]

                def mod(b, par, first=False):
                    act.wait_ge(s["zT"], b + 1)
                    if not first:
                        act.wait_ge(s["hT"], b - 1)
                        if NX[n]:
                            act.wait_ge(s["x"], b - 1)
                    act.activation(hcur[:, par, :], bank[par][:, 0:T], ACT.Identity,
                                   bias=modT[l][:, sh, bass.ds(b, 1)],
                                   scale=modT[l][:, sc, bass.ds(b, 1)]).then_inc(s["h"], 1)

                def gelu(b, par):
                    act.wait_ge(s["xin"], b + 1)
                    act.activation(xt[:, par, :, 0:HID], xt[:, par, :, 0:HID], ACT.Gelu).then_inc(s["gelu"], 1)

                def one(b, par, first=False, lag=True):
                    mod(b, par, first)
                    if n == 0 and lag:
                        gelu(b - 1, 1 - par)

                one(0, 0, True, False)
                one(1, 1, True)
                with act.Fori(1, B // 2) as i:
                    for par in range(2):
                        one(2 * i + par, par)
                if n == 0:
                    gelu(B - 1, 1)

            act.wait_ge(mod_cp, 2)
            norm(0)
            act.wait_ge(gl_in, 1)
            act.activation(gl[:], gl[:], ACT.Exp, scale=-1.0)
            act.activation(gs[:], gst[:], ACT.Exp, scale=-1.0)
            act.drain().then_inc(gl_exp, 1)
            phase(act, 1)

            def attention(l):
                s = att_s[l]
                W = 512 if l == 0 else 384

                def prep(b, par, first=False, which=(0, 1)):
                    n = 3 if l else 2
                    if not first:
                        act.wait_ge(s["qz"], 2 * b)
                    for i, dst in enumerate([qsT[:], ksT[:, par]]):
                        if i not in which:
                            continue
                        act.wait_ge(s["sT"], n * b + i + 1)
                        act.activation(dst.rearrange("p j t -> p (j t)"),
                                       M[:, i, :].bitcast(F16), ACT.Copy).then_inc(s["sE"], 1)

                def prep_again(b, par):
                    if l:
                        act.wait_ge(s["sT"], 3 * b + 3)
                        act.activation(qsT[:].rearrange("p j t -> p (j t)"),
                                       M[:, 0, :].bitcast(F16), ACT.Copy).then_inc(s["sE"], 1)

                def tail_o(b, i, first=False):
                    act.wait_ge(s["pv"], CH * b + 4 * i + 4)
                    if i == 0 and not first:
                        act.wait_ge(s["oT"], 2 * b)
                    act.activation(oT[:].rearrange("p j t -> p (j t)")[:, i * 512:i * 512 + 512],
                                   OP[:, i, :], ACT.Copy).then_inc(s["o"], 1)

                def tail_a(b):
                    act.wait_ge(s["aT"], b + 1)
                    act.activation(aT[:], OP[:, 1, 0:T], ACT.Copy).then_inc(s["aE"], 1)

                def exp(b, u, first=False):
                    act.wait_ge(s["score"], CH * b + u + 1)
                    if not (first and u < 4):
                        act.wait_ge(s["pv"], CH * b + u - 3)
                    act.activation(pt[:, u % 4, :, 0:W], SP[u % 2][:, :, 0:W], ACT.Exp,
                                   scale=SCALE).then_inc(s["exp"], 1)

                def one(b, par, first=False, tail=True, nxt=True):
                    for u in range(CH):
                        exp(b, u, first)
                        if u == 0 and tail:
                            tail_o(b - 1, 1)
                        if u == 4 and tail:
                            tail_a(b - 1)
                        if l and u == 1 and nxt:
                            prep(b + 1, 1 - par)
                        if l == 0 and u in (5, 6) and nxt:
                            prep(b + 1, 1 - par, which=(u - 5,))
                        if u == 6:
                            tail_o(b, 0, first)
                    if nxt:
                        prep_again(b + 1, 1 - par)

                prep(0, 0, True)
                prep_again(0, 0)
                one(0, 0, True, tail=False)
                one(1, 1)
                with act.Fori(1, B // 2 - 1) as i:
                    for par in range(2):
                        one(2 * i + par, par)
                one(B - 2, 0)
                one(B - 1, 1, nxt=False)
                tail_o(B - 1, 1)
                tail_a(B - 1)

            def router():
                act.wait_ge(norm_s[1]["rexp"], 1)

            def experts(l, E, F):
                s = exp_s[l]

                def one(g, par, first=False):
                    for e in range(E):
                        for f in range(F):
                            k = e * F + f
                            act.wait_ge(s["hid"], E * F * g + k + 1)
                            if f == 0 and not (first and par == 0 and e < 2):
                                act.wait_ge(s["y"], E * g + e - 1)
                            act.activation(hid[:, e % 2, f, :], bank[k % 4], ACT.Relu,
                                           bias=b1[l][:, k:k + 1]).then_inc(s["relu"], 1)

                one(0, 0, True)
                one(1, 1, True)
                with act.Fori(1, NG // 2) as i:
                    for par in range(2):
                        one(2 * i + par, par)

            attention(0)
            phase(act, 2)
            norm(1)
            act.wait_ge(norm_s[1]["rexp"], 1)
            act.activation(rt[:, :, 0:E0], rt[:, :, 0:E0], ACT.Exp).then_inc(norm_s[1]["gelu"], 1)
            phase(act, 3)
            experts(0, E0, F0)
            phase(act, 4)
            norm(2)
            phase(act, 5)
            attention(1)
            phase(act, 6)
            norm(3)
            act.wait_ge(norm_s[3]["rexp"], 1)
            act.activation(rt[:, :, 0:E1], rt[:, :, 0:E1], ACT.Exp).then_inc(norm_s[3]["gelu"], 1)
            phase(act, 7)
            experts(1, E1, F1)
            phase(act, 8)

        @block.vector
        def _(dve):
            dve.wait_ge(silu_e, 2)
            for l in range(2):
                dve.tensor_scalar(ce[l][:], ce[l][:], 1.0, None, ALU.add)
            dve.drain()
            for l in range(2):
                dve.reciprocal(ce[l][:], ce[l][:])
            dve.drain()
            for l in range(2):
                dve.tensor_tensor(ce[l][:], ce[l][:], cT[l][:], ALU.mult).then_inc(silu_r, 1)
            for l in range(2):
                dve.wait_ge(mod_mm, l + 1)
                dve.tensor_copy(modT[l][:].rearrange("p m b -> p (m b)"), bank[l][:, 0:6 * B])
            dve.drain()
            for l in range(2):
                dve.tensor_scalar(modT[l][:, CA, :], modT[l][:, CA, :], 1.0, None, ALU.add)
                dve.tensor_scalar(modT[l][:, CB, :], modT[l][:, CB, :], 1.0, None, ALU.add).then_inc(mod_cp, 1)
            dve.wait_ge(g_mm, 1)
            dve.tensor_copy(graw.rearrange("p n d -> p (n d)"), bank[2][0:B, :])
            dve.drain()
            flat = [v.rearrange("p n d -> p (n d)") for v in (graw, gsign, gmag)]
            dve.tensor_scalar(flat[1], flat[0], 0.0, 2.0, ALU.is_ge, ALU.mult)
            dve.scalar_tensor_tensor(flat[2], flat[0], -1.0, flat[0], ALU.mult, ALU.max)
            dve.drain()
            dve.tensor_scalar(flat[2], flat[2], 0.25, None, ALU.max)
            dve.drain()
            dve.scalar_tensor_tensor(flat[0], flat[1], -1.0, flat[2], ALU.add, ALU.mult).then_inc(g_fin, 1)

            def guess(y, x):
                yi = y.bitcast(I32)
                dve.tensor_scalar(yi, x.bitcast(I32), 1, None, ALU.logical_shift_right)
                dve.drain()
                return dve.tensor_scalar(yi, yi, -1.0, float(0x5F3759DF), ALU.mult, ALU.add)

            def rsqrt(y, x, t):
                guess(y, x)
                for _ in range(3):
                    dve.drain()
                    dve.tensor_tensor(t, y, y, ALU.mult)
                    dve.drain()
                    dve.scalar_tensor_tensor(t, t, -0.5, x, ALU.mult, ALU.mult)
                    dve.drain()
                    dve.scalar_tensor_tensor(y, t, 1.5, y, ALU.add, ALU.mult)
                dve.drain()

            def norm(n):
                s = norm_s[n]

                if n == 0:
                    for i in range(8):
                        dve.wait_ge(x_in[i], 16)
                        for k in range(8):
                            dve.bn_stats(stats[:, 8 * i + k, :], x_sb[:, 8 * i + k, :])
                else:
                    with dve.Fori(0, NT // 8) as i:
                        for k in range(8):
                            dve.bn_stats(stats[:, 8 * i + k, :], x_sb[:, 8 * i + k, :])
                dve.drain()
                dve.tensor_tensor(mean[:], stats[:, :, 1], stats[:, :, 4], ALU.add)
                dve.tensor_tensor(dev[:], stats[:, :, 1], stats[:, :, 4], ALU.subtract)
                dve.tensor_tensor(var[:], stats[:, :, 2], stats[:, :, 5], ALU.add)
                dve.drain()
                dve.tensor_scalar(mean[:], mean[:], 0.5, None, ALU.mult)
                dve.tensor_tensor(dev[:], dev[:], dev[:], ALU.mult)
                dve.tensor_scalar(var[:], var[:], 1.0 / D, LN_EPS, ALU.mult, ALU.add)
                dve.drain()
                dve.scalar_tensor_tensor(var[:], dev[:], 0.25, var[:], ALU.mult, ALU.add)
                dve.drain()
                rsqrt(rstd[:], var[:], dev[:])

                def ln(b, par, first=False):
                    if not first:
                        dve.wait_ge(s["zT"], b - 1)
                    for t in range(TT):
                        k = bass.ds(2 * b + t, 1)
                        dve.tensor_scalar(z[:, par, t, :], x_sb[:, 2 * b + t, :], mean[:, k],
                                          rstd[:, k], ALU.subtract, ALU.mult).then_inc(s["z"], 1)

                def extra(b, par):
                    if n == 2:
                        return
                    dve.wait_ge(s["x"], b + 1)
                    nx = NX[n]
                    src = bank[2 + par][:, 0:TT * nx].rearrange("p (t x) -> p t x", t=TT)
                    bias = bx[n][:].unsqueeze(1).to_broadcast([P, TT, nx])
                    if n == 3:
                        dve.tensor_tensor(logit[1][:, bass.ts(b, TT), :], src, bias, ALU.add).then_inc(s["xin"], 1)
                        return
                    dve.tensor_tensor(xt[:, par, :, 0:nx], src, bias, ALU.add).then_inc(s["xin"], 1)
                    if n == 0:
                        return
                    dve.drain()
                    dve.tensor_copy(logit[0][:, bass.ts(b, TT), :], xt[:, par, :, 0:E0])
                    for t in range(TT):
                        dve.scalar_tensor_tensor(xt[:, par, t, E0:nx], xt[:, par, t, E0:nx], 0.0, dpw2[:],
                                                 ALU.max, ALU.mult, accum_out=zdp[:, 2 * b + t, :])
                    dve.drain()

                def sums(b, par):
                    if n == 0:
                        dve.wait_ge(s["gmm"], b + 1)
                        dve.tensor_copy(gsum[:, bass.ds(b, 1)], bank[4 + par][0:HID, 0:1]).then_inc(s["gsum"], 1)

                def one(b, par, first=False, lag=1):
                    ln(b, par, first)
                    if lag:
                        extra(b - 1, 1 - par)
                    if lag > 1:
                        sums(b - 2, par)

                one(0, 0, True, 0)
                one(1, 1, True, 1)
                with dve.Fori(1, B // 2) as i:
                    for par in range(2):
                        one(2 * i + par, par, False, 2)
                extra(B - 1, 1)
                sums(B - 2, 0)
                sums(B - 1, 1)

            norm(0)
            dve.wait_ge(gl_mm, 1)
            dve.scalar_tensor_tensor(gl[:], bank[6][0:B, 0:H], 1.0 / T, bg2[:], ALU.mult, ALU.add).then_inc(gl_in, 1)
            dve.wait_ge(gl_exp, 1)
            dve.tensor_scalar(gl[:], gl[:], 1.0, None, ALU.add)
            dve.drain()
            dve.scalar_tensor_tensor(gs[:], gs[:], 1.0, gl[:], ALU.add, ALU.mult)
            dve.drain()
            dve.reciprocal(gs[:], gs[:]).then_inc(gl_fin, 1)
            dve.wait_ge(gate_in, 16)
            dve.wait_ge(row_in, 16)
            phase(dve, 1)

            def attention(l):
                s = att_s[l]

                def prep_qkv(b, first=False):
                    if not first:
                        dve.wait_ge(s["vs"], b)
                        dve.wait_ge(s["stack"], 2 * b)
                    for t in range(TT):
                        dve.wait_ge(s["proj"], 2 * b + t + 1)
                        src = M[:, 1 - t if l else t, 0:3 * D].rearrange("p (w d) -> p w d", w=3)
                        if l == 0:
                            dve.tensor_tensor(qkv[:, :, t, :], src, bqkv[:].rearrange("p (w d) -> p w d", w=3),
                                              ALU.add)
                        else:
                            dve.tensor_copy(qkv[:, :, t, :], src)
                    dve.drain().then_inc(s["qkv"], 1)
                    if l == 0:
                        flat = qk.rearrange("p w t d -> p (w t d)")
                        dve.tensor_tensor(sq[:].rearrange("p w t d -> p (w t d)"), flat, flat, ALU.mult)
                        dve.drain()
                        dve.tensor_reduce(n2[:], sq[:].rearrange("p w t (h d) -> p (w t h) d", d=DH), AX.X, ALU.add)
                        dve.drain()
                        dve.tensor_scalar(n2[:], n2[:], NORM_EPS ** 2, None, ALU.max)
                        dve.drain()
                        guess(rn[:, :, 0], n2[:, :, 0]).then_inc(s["guess"], 1)

                def prep_split(b, first=False):
                    heads = qk.rearrange("p w t (h d) -> p (w t h) d", d=DH)
                    if l == 0:
                        dve.wait_ge(s["rn"], b + 1)
                        dve.tensor_tensor(heads, heads, rn[:].to_broadcast([P, 2 * TT * H, DH]), ALU.mult)
                        dve.drain()
                    if not first:
                        dve.wait_ge(s["sT"], (3 if l else 2) * b)
                    for w in range(2):
                        src = heads[:, w * TT * H:(w + 1) * TT * H, :]
                        hi = st[:, 0, :, 0:3:2, :] if w == 0 else st[:, 1, :, 0:2, :]
                        dve.tensor_copy(hi, src.unsqueeze(2).to_broadcast([P, TT * H, 2, DH]))
                    dve.drain()
                    for w in range(2):
                        src = heads[:, w * TT * H:(w + 1) * TT * H, :]
                        top = st[:, w, :, 0, :]
                        if l == 0:
                            lo = st[:, 0, :, 1:4:2, :] if w == 0 else st[:, 1, :, 2:4, :]
                            ins = dve.tensor_tensor(lo, src.unsqueeze(2).to_broadcast([P, TT * H, 2, DH]),
                                                    top.unsqueeze(2).to_broadcast([P, TT * H, 2, DH]), ALU.subtract)
                        else:
                            lo = st[:, 0, :, 1, :] if w == 0 else st[:, 1, :, 2, :]
                            ins = dve.tensor_tensor(lo, src, top, ALU.subtract)
                        ins.then_inc(s["stack"], 1)

                def prep_max(b, k):
                    dve.wait_ge(s["mfill"], 12 * b + k + 1)
                    jj, g = k // 4, k % 4
                    to = mx[:, 1, 2 * jj:2 * jj + 2, g:g + 1] if k < 8 else mx[:, 0, :, g:g + 1]
                    dve.tensor_reduce(to, M[:, k % 2, :].rearrange("p (j k) -> p j k", j=2 if k < 8 else 4),
                                      AX.X, ALU.max).then_inc(s["mred"], 1)

                def prep_row(b):
                    dve.drain()
                    dve.tensor_scalar(st[:, 0, :, 3, 0:1], mx[:].rearrange("p t j g -> p (t j g)").unsqueeze(2),
                                      -1.0 / MSHIFT, None, ALU.mult).then_inc(s["mrow"], 1)

                def prep_heads(b, par, first=False):
                    dve.wait_ge(s["sE"], 3 * b + 3 if l else 2 * b + 1)
                    if not first:
                        dve.wait_ge(s["score"], CH * (b - 1))
                    for half in range(2):
                        for g in (2 * half, 2 * half + 1):
                            rows32 = slice(32 * g, 32 * g + 32)
                            last = dve.tensor_copy(qz[rows32, par, g], qsT[rows32])
                        last.then_inc(s["qz"], 1)

                def tail_n(b, t):
                    dve.wait_ge(s["oT"], 2 * b + t + 1)
                    o = OP[:, 1].rearrange("p (h c) -> p h c", c=32)
                    r = rs[:, t * H:(t + 1) * H, :]
                    dve.reciprocal(r, o[:, :, DH:DH + 1])
                    dve.drain()
                    if l == 0:
                        dve.tensor_tensor(r.rearrange("p h o -> p o h"), r.rearrange("p h o -> p o h"),
                                          gateB[:, bass.ds(b, 1), :], ALU.mult)
                        dve.drain()
                    dve.tensor_tensor(an[:, t * H:(t + 1) * H, :], o[:, :, 0:DH], r.to_broadcast([P, H, DH]),
                                      ALU.mult).then_inc(s["an"], 1)

                def tail_x(b):
                    dve.wait_ge(s["wo"], b + 1)
                    w = OP[:, 1, T:T + TT * D].rearrange("p (t d) -> p t d", t=TT)
                    ga = rows[:, bass.ds(b, 1), :].to_broadcast([P, TT, D])
                    if l == 0:
                        dve.tensor_tensor(ao[:], w, bo[:].unsqueeze(1).to_broadcast([P, TT, D]),
                                          ALU.add).then_inc(s["wr"], 1)
                        dve.drain()
                        dve.tensor_tensor(ao[:], ao[:], ga, ALU.mult)
                    else:
                        dve.tensor_tensor(ao[:], w, ga, ALU.mult).then_inc(s["wr"], 1)
                    dve.drain()
                    xs = x_sb[:, bass.ts(b, TT), :]
                    dve.tensor_tensor(xs, xs, ao[:], ALU.add).then_inc(s["x"], 1)

                def one(b, par, tail=True, nxt=True, nxt2=True, first=False):
                    if l == 0:
                        if nxt:
                            prep_split(b + 1)
                        if tail:
                            tail_n(b - 1, 0)
                            tail_n(b - 1, 1)
                        if nxt2:
                            prep_qkv(b + 2)
                        if tail:
                            tail_x(b - 1)
                    else:
                        for k in range(12):
                            if k in (0, 3) and tail:
                                tail_n(b - 1, k // 3)
                            if k == 9 and tail:
                                tail_x(b - 1)
                            if nxt:
                                prep_max(b + 1, k)
                        if nxt:
                            prep_row(b + 1)
                    if nxt:
                        prep_heads(b + 1, 1 - par, first)
                    if l and nxt2:
                        prep_qkv(b + 2)
                        prep_split(b + 2)

                prep_qkv(0, True)
                prep_split(0, True)
                if l:
                    for k in range(12):
                        prep_max(0, k)
                    prep_row(0)
                prep_qkv(1)
                prep_heads(0, 0, True)
                if l:
                    prep_split(1)
                one(0, 0, tail=False, first=True)
                one(1, 1)
                with dve.Fori(1, B // 2 - 1) as i:
                    for par in range(2):
                        one(2 * i + par, par)
                one(B - 2, 0, nxt2=False)
                one(B - 1, 1, nxt=False, nxt2=False)
                tail_n(B - 1, 0)
                tail_n(B - 1, 1)
                tail_x(B - 1)

            def route(n, l, E):
                s = norm_s[n]
                dve.drain()
                if l == 0:
                    for k, (cut, op) in enumerate(K_CUTS):
                        dst = kt if k == 0 else rm
                        dve.tensor_scalar(dst[:], zdp[:], dpb2[:, 0:1], cut, ALU.add, op)
                        dve.drain()
                        if k:
                            dve.tensor_tensor(kt[:], kt[:], rm[:], ALU.add)
                            dve.drain()
                    dve.tensor_scalar(kt[:], kt[:], 1.0, None, ALU.add)
                L = logit[l]
                dve.tensor_reduce(rm[:], L[:], AX.X, ALU.max)
                dve.memset(rank[:, :, 0:E], 0.0)
                dve.drain()
                for o in range(E):
                    other = L[:, :, o:o + 1]
                    if o + 1 < E:
                        dve.tensor_tensor(rt[:, :, o + 1:E], other.to_broadcast([P, NT, E - o - 1]),
                                          L[:, :, o + 1:E], ALU.is_ge)
                    if o:
                        dve.tensor_tensor(rt[:, :, 0:o], other.to_broadcast([P, NT, o]), L[:, :, 0:o], ALU.is_gt)
                    dve.drain()
                    if o + 1 < E:
                        dve.tensor_tensor(rank[:, :, o + 1:E], rank[:, :, o + 1:E], rt[:, :, o + 1:E], ALU.add)
                    if o:
                        dve.tensor_tensor(rank[:, :, 0:o], rank[:, :, 0:o], rt[:, :, 0:o], ALU.add)
                    dve.drain()
                kept = kt[:].to_broadcast([P, NT, E]) if l == 0 else None
                if l == 0:
                    dve.tensor_tensor(rank[:, :, 0:E], rank[:, :, 0:E], kept, ALU.is_lt)
                else:
                    dve.tensor_scalar(rank[:, :, 0:E], rank[:, :, 0:E], 2.0, None, ALU.is_lt)
                dve.tensor_tensor(rt[:, :, 0:E], L[:], rm[:].to_broadcast([P, NT, E]), ALU.subtract)
                dve.drain().then_inc(s["rexp"], 1)
                dve.wait_ge(s["gelu"], 1)
                dve.tensor_tensor(rt[:, :, 0:E], rt[:, :, 0:E], rank[:, :, 0:E], ALU.mult)
                dve.drain()
                dve.tensor_reduce(rm[:], rt[:, :, 0:E], AX.X, ALU.add)
                dve.drain()
                dve.reciprocal(rm[:], rm[:])
                dve.drain()
                dve.tensor_tensor(comb[l][:], rt[:, :, 0:E], rm[:].to_broadcast([P, NT, E]), ALU.mult)

            def experts(l, E, F):
                s = exp_s[l]

                def one(g, par):
                    dve.wait_ge(s["cT"], g + 1)
                    dve.tensor_copy(cTr[l][:], bank[7][0:E, :]).then_inc(s["cE"], 1)
                    dve.wait_ge(s["b2"], g + 1)
                    dve.tensor_copy(acc.rearrange("p t d -> p (t d)"), bank[6])
                    dve.drain()
                    for e in range(E):
                        dve.wait_ge(s["y"], E * g + e + 1)
                        for t in range(GT):
                            dve.scalar_tensor_tensor(acc[:, t, :], bank[4 + e % 2][:, t * D:(t + 1) * D],
                                                     ccur[l][:, par, t, e:e + 1], acc[:, t, :], ALU.mult, ALU.add)
                        dve.drain().then_inc(s["acc"], 1)
                    for k in range(2):
                        v = acc[:, 2 * k:2 * k + 2, :]
                        dve.tensor_tensor(v, v, rows[:, bass.ds(2 * g + k, 1), :].to_broadcast([P, TT, D]), ALU.mult)
                    dve.drain()
                    xs = x_sb[:, bass.ts(g, GT), :]
                    dve.tensor_tensor(xs, xs, acc, ALU.add).then_inc(s["done"], 1)

                with dve.Fori(0, NG // 2) as i:
                    for par in range(2):
                        one(2 * i + par, par)

            attention(0)
            phase(dve, 2)
            norm(1)
            route(1, 0, E0)
            dve.wait_ge(row_in, 32)
            phase(dve, 3)
            experts(0, E0, F0)
            phase(dve, 4)
            norm(2)
            dve.wait_ge(row_in, 48)
            phase(dve, 5)
            attention(1)
            phase(dve, 6)
            norm(3)
            route(3, 1, E1)
            dve.wait_ge(row_in, 64)
            phase(dve, 7)
            experts(1, E1, F1)
            phase(dve, 8)

        @block.tensor
        def _(pe):
            pe.wait_ge(idents, 1)
            pe.wait_ge(w_in, 16 * (len(FIRST) + len(LOADS)))
            for l in range(2):
                pe.wait_ge(silu_r, l + 1)
                for m in range(6):
                    last = pe.matmul(bank[l][:, m * B:(m + 1) * B], wmod[l][:, m * D:(m + 1) * D], ce[l][:],
                                     start=True, stop=True)
                last.then_inc(mod_mm, 1)
            for n in range(4):
                l, m = n // 2, (GA, GB)[n % 2]
                last = pe.matmul(bank[2][0:B, n * D:(n + 1) * D], ce[l][:], wmod[l][:, m * D:(m + 1) * D],
                                 start=True, stop=True)
            last.then_inc(g_mm, 1)
            pe.wait_ge(mod_cp, 2)
            pe.wait_ge(g_fin, 1)

            def norm(n):
                s = norm_s[n]

                def turn(b, par, first=False):
                    if not first:
                        pe.wait_ge(s["h"], b - 1)
                    for t in range(TT):
                        pe.wait_ge(s["z"], TT * b + t + 1)
                        last = pe.transpose(bank[par][:, t * P:(t + 1) * P], z[:, par, t, :], ident[:])
                    last.then_inc(s["zT"], 1)

                def project(b, par, first=False):
                    if not NX[n]:
                        return
                    pe.wait_ge(s["h"], b + 1)
                    if not first:
                        pe.wait_ge(s["xin"], b - 1)
                    for t in range(TT):
                        last = pe.matmul(bank[2 + par][:, t * NX[n]:(t + 1) * NX[n]],
                                         hcur[:, par, t * P:(t + 1) * P], wx[n][:], start=True, stop=True)
                    last.then_inc(s["x"], 1)

                def gate_sum(b, par, first=False):
                    if n:
                        return
                    pe.wait_ge(s["gelu"], b + 1)
                    if not first:
                        pe.wait_ge(s["gsum"], b - 1)
                    for t in range(TT):
                        last = pe.matmul(bank[4 + par][0:HID, 0:1], xt[:, par, t, 0:HID], ones[:],
                                         start=(t == 0), stop=(t == TT - 1))
                    last.then_inc(s["gmm"], 1)

                turn(0, 0, True)
                turn(1, 1, True)
                project(0, 0, True)
                turn(2, 0)
                project(1, 1, True)
                gate_sum(0, 0, True)
                turn(3, 1)
                project(2, 0)
                gate_sum(1, 1, True)
                with pe.Fori(2, B // 2) as i:
                    for par in range(2):
                        turn(2 * i + par, par)
                        project(2 * i + par - 1, 1 - par)
                        gate_sum(2 * i + par - 2, par)
                project(B - 1, 1)
                gate_sum(B - 2, 0)
                gate_sum(B - 1, 1)

            norm(0)
            pe.wait_ge(norm_s[0]["gsum"], B)
            pe.matmul(bank[6][0:B, 0:H], gsum[:], wg2[:], start=True, stop=True).then_inc(gl_mm, 1)
            phase(pe, 1)

            def attention(l):
                s = att_s[l]
                per = 3 if l else 2

                def prep_proj(b, first=False, values_between=None):
                    pe.wait_ge(s["h"], b + 1)
                    for t in range(TT):
                        pe.matmul(M[:, 1 - t if l else t, 0:3 * D], ha[:, t * P:(t + 1) * P], wqkv[l][:],
                                  start=True, stop=True).then_inc(s["proj"], 1)
                        if values_between and t == 0:
                            values_between()
                        if l and t == 0 and not first:
                            pe.wait_ge(s["sE"], 3 * b)

                def turn_stack(b, w, bankno):
                    to = M[:, bankno, :].bitcast(F16)
                    for j in range(NJ):
                        for t in range(TT):
                            src = st[:, w, t * H + j * HG:t * H + (j + 1) * HG].rearrange("p h r d -> p (h r d)")
                            last = pe.transpose(to[:, j * T + t * P:j * T + (t + 1) * P], src, ident16[:])
                    last.then_inc(s["sT"], 1)

                def prep_turn(b, drained):
                    pe.wait_ge(s["qkv"], drained)
                    for w in range(2):
                        pe.wait_ge(s["stack"], 2 * b + w + 1)
                        turn_stack(b, w, w)

                def prep_max(b, par, k):
                    if k == 0:
                        pe.wait_ge(s["sE"], per * b + 2)
                    if k >= 2:
                        pe.wait_ge(s["mred"], 12 * b + k - 1)
                    to, g = M[:, k % 2, :], k % 4
                    if k < 8:
                        v = to.rearrange("p (j k) -> p j k", j=2)
                        pe.matmul(v[:, :, P:T], identb[:], maskQ[:].unsqueeze(1).to_broadcast([P, 2, P]),
                                  start=True, stop=False, skip_group_check=True)
                        js, q0, kn = (2 * (k // 4), 2 * (k // 4) + 1), P, T
                    else:
                        v = to.rearrange("p (j k) -> p j k", j=4)
                        pe.matmul(v[:, :, :], identb[:], maskQ[:].unsqueeze(1).to_broadcast([P, 4, P]),
                                  start=True, stop=False, skip_group_check=True)
                        js, q0, kn = range(4), 0, P
                    for n, j in enumerate(js):
                        last = pe.matmul(v[:, n, :], qsT[32 * g:32 * g + 3 * DH, j, q0:q0 + P],
                                         ksT[32 * g:32 * g + 3 * DH, par, j, 0:kn], start=False, stop=True,
                                         skip_group_check=True, tile_position=(32 * g, 0))
                    last.then_inc(s["mfill"], 1)

                def prep_requeue(b):
                    pe.wait_ge(s["mrow"], b + 1)
                    turn_stack(b, 0, 0)

                def score(b, par, u, first=False):
                    if u == 0:
                        pe.wait_ge(s["sE"], per * b + 2)
                    if u < 2:
                        pe.wait_ge(s["qz"], 2 * b + u + 1)
                    if not (first and u < 2):
                        pe.wait_ge(s["exp"], CH * b + u - 1)
                    j = u // 2
                    for i in range(2):
                        g = 2 * (u % 2) + i
                        to = SP[u % 2][:, i, :]
                        for k in range(TT):
                            q0 = P if (l and k) else 0
                            last = pe.matmul(to[:, k * T:k * T + T - q0],
                                             ksT[:, par, j, k * P:(k + 1) * P], qz[:, par, g, j, q0:T],
                                             start=True, stop=True)
                    last.then_inc(s["score"], 1)

                def values(b, par, u, first=False):
                    if u == 0:
                        pe.wait_ge(s["vs"], b + 1)
                    pe.wait_ge(s["sel" if l else "exp"], CH * b + u + 1)
                    if not first and u % 4 == 0:
                        pe.wait_ge(s["o"], 2 * b + u // 4 - 1)
                        if u:
                            pe.wait_ge(s["wr"], b)
                    j = u // 2
                    for k in range(TT):
                        q0 = P if (l and k) else 0
                        for i in range(2):
                            g = 2 * (u % 2) + i
                            c = (j % 2) * T
                            last = pe.matmul(OP[32 * g:32 * g + 32, j // 2, c + q0:c + T],
                                             vs[:, par, k, HG * j + g, :],
                                             pt[:, u % 4, i, k * T:k * T + T - q0],
                                             start=(k == 0), stop=(k == TT - 1),
                                             skip_group_check=True, tile_position=(0, 32 * g))
                    last.then_inc(s["pv"], 1)

                def tail_turn(b, t):
                    if t == 0:
                        pe.wait_ge(s["o"], 2 * b + 2)
                    if t:
                        pe.wait_ge(s["an"], 2 * b + 1)
                    to = OP[:, 1]
                    for j in range(NJ):
                        last = pe.transpose(to[:, j * P:(j + 1) * P], oT[:, j, t * P:(t + 1) * P], ident[:])
                    last.then_inc(s["oT"], 1)

                def tail_an(b):
                    pe.wait_ge(s["an"], 2 * b + 2)
                    to = OP[:, 1]
                    for t in range(TT):
                        last = pe.transpose(to[:, t * P:(t + 1) * P],
                                            an[:, t * H:(t + 1) * H, :].rearrange("p h d -> p (h d)"), ident[:])
                    last.then_inc(s["aT"], 1)

                def tail_wo(b):
                    pe.wait_ge(s["aE"], b + 1)
                    to = OP[:, 1, T:T + TT * D]
                    for t in range(TT):
                        last = pe.matmul(to[:, t * D:(t + 1) * D], aT[:, t * P:(t + 1) * P], wo[l][:],
                                         start=True, stop=True)
                    last.then_inc(s["wo"], 1)

                def one0(b, par, first=False, tail=True, nxt=True, nxt2=True):
                    for u in range(CH):
                        score(b, par, u, first)
                        if tail and u in (2, 3):
                            tail_turn(b - 1, u - 2)
                        if tail and u == 4:
                            tail_an(b - 1)
                        if tail and u == 5:
                            tail_wo(b - 1)
                        if tail and u == 0:
                            values(b - 1, 1 - par, CH - 1)
                        if u >= 2:
                            values(b, par, u - 2, first)
                        if nxt2 and u == 3:
                            pe.wait_ge(s["sE"], 2 * b + 2)
                            prep_proj(b + 2)
                        if nxt and u == 5:
                            prep_turn(b + 1, b + 3 if nxt2 else b + 2)
                    values(b, par, CH - 2, first)

                FILLS = [0, 0, 2, 3, 2, 2, 2, 1]

                def one1(b, par, first=False, tail=True, nxt=True, nxt2=True):
                    done = 0
                    for u in range(CH):
                        score(b, par, u, first)
                        for k in range(done, done + FILLS[u]):
                            if tail and k == 0:
                                tail_turn(b - 1, 0)
                            if tail and k == 3:
                                tail_turn(b - 1, 1)
                            if tail and k == 5:
                                tail_an(b - 1)
                            if tail and k == 7:
                                tail_wo(b - 1)
                            if nxt:
                                prep_max(b + 1, 1 - par, k)
                        done += FILLS[u]
                        if tail and u == 0:
                            values(b - 1, 1 - par, CH - 1)
                        if u >= 2:
                            values(b, par, u - 2, first)
                        if nxt and u == 1:
                            prep_turn(b + 1, b + 2)
                    if nxt:
                        prep_requeue(b + 1)
                    if nxt2:
                        pe.wait_ge(s["mred"], 12 * (b + 2))
                        prep_proj(b + 2, values_between=lambda: values(b, par, CH - 2, first))
                    else:
                        values(b, par, CH - 2, first)

                one = one1 if l else one0
                prep_proj(0, True)
                if l == 0:
                    pe.wait_ge(s["qkv"], 1)
                    prep_proj(1)
                    prep_turn(0, 2)
                else:
                    prep_turn(0, 1)
                    for k in range(12):
                        prep_max(0, 0, k)
                    prep_requeue(0)
                    pe.wait_ge(s["mred"], 12)
                    prep_proj(1)
                one(0, 0, True, tail=False)
                one(1, 1)
                with pe.Fori(1, B // 2 - 1) as i:
                    for par in range(2):
                        one(2 * i + par, par)
                one(B - 2, 0, nxt2=False)
                one(B - 1, 1, nxt=False, nxt2=False)
                values(B - 1, 1, CH - 1)
                pe.wait_ge(s["wr"], B - 1)
                tail_turn(B - 1, 0)
                tail_turn(B - 1, 1)
                tail_an(B - 1)
                tail_wo(B - 1)

            def experts(l, E, F):
                s = exp_s[l]
                N = GT * P

                def weights(g, par):
                    pe.wait_ge(s["c"], g + 1)
                    for t in range(GT):
                        last = pe.transpose(bank[7][0:E, t * P:(t + 1) * P], ccur[l][:, par, t, :], ident[:])
                    last.then_inc(s["cT"], 1)

                def bias2(g, first):
                    pe.wait_ge(s["cE"], g + 1)
                    if not first:
                        pe.wait_ge(s["acc"], E * g)
                    for t in range(GT):
                        last = pe.matmul(bank[6][:, t * D:(t + 1) * D], cTr[l][:, t * P:(t + 1) * P], b2[l][:],
                                         start=True, stop=True)
                    last.then_inc(s["b2"], 1)

                def hidden(g, e, first):
                    for f in range(F):
                        k = e * F + f
                        if not (first and k < 4):
                            pe.wait_ge(s["relu"], E * F * g + k - 3)
                        pe.matmul(bank[k % 4], w1[l][:, e, f * P:(f + 1) * P], hT[:, bass.ts(g, N)],
                                  start=True, stop=True).then_inc(s["hid"], 1)

                def outputs(g, e, first):
                    pe.wait_ge(s["relu"], E * F * g + (e + 1) * F)
                    if not (first and e < 2):
                        pe.wait_ge(s["acc"], E * g + e - 1)
                    for t in range(GT):
                        for f in range(F):
                            last = pe.matmul(bank[4 + e % 2][:, t * D:(t + 1) * D],
                                             hid[:, e % 2, f, t * P:(t + 1) * P], w2[l][:, e * F + f, :],
                                             start=(f == 0), stop=(f == F - 1))
                    last.then_inc(s["y"], 1)

                def one(g, par, first=False):
                    weights(g, par)
                    for e in range(E):
                        hidden(g, e, first)
                        if e == 0:
                            bias2(g, first)
                        else:
                            outputs(g, e - 1, first)
                    outputs(g, E - 1, first)

                one(0, 0, True)
                one(1, 1)
                with pe.Fori(1, NG // 2) as i:
                    for par in range(2):
                        one(2 * i + par, par)

            attention(0)
            phase(pe, 2)
            norm(1)
            phase(pe, 3)
            pe.wait_ge(late_in, 16 * len(LATE))
            experts(0, E0, F0)
            phase(pe, 4)
            norm(2)
            phase(pe, 5)
            attention(1)
            phase(pe, 6)
            norm(3)
            phase(pe, 7)
            pe.wait_ge(late_in, 16 * (len(LATE) + len(LAST)))
            experts(1, E1, F1)
            phase(pe, 8)


def layout(i):
    import numpy as np

    def c(v):
        return np.ascontiguousarray(v)

    def rep(v, n=P):
        return c(np.broadcast_to(np.asarray(v).reshape(1, -1), (n, np.asarray(v).size)))

    def experts(w, b, w2, b2, e, f):
        return (c(np.transpose(w, (1, 0, 2))),
                c(np.transpose(np.asarray(w2).reshape(e * f, P, D), (1, 0, 2))),
                c(np.asarray(b).reshape(e * f, P).T), c(b2))

    i = {k: np.asarray(v) for k, v in i.items()}
    a = {"x": c(i["L0_attn_x"])}
    for l in range(2):
        a[f"cT{l}"] = c(i[f"L{l}_c"].T)
        a[f"wmod{l}"] = c(i[f"L{l}_wmod"])
    a["wqkv0"] = c(np.concatenate([i["L0_attn_Wq"].T, i["L0_attn_Wk"].T, i["L0_attn_Wv"].T], axis=1))
    a["wqkv1"] = c(np.concatenate([i["L1_attn_Wq"], i["L1_attn_Wkv"]], axis=1))
    a["wo0"], a["wo1"] = c(i["L0_attn_Wo"].T), c(i["L1_attn_Wo"])
    a["bqkv0"] = rep(np.concatenate([i["L0_attn_bq"], i["L0_attn_bk"], i["L0_attn_bv"]]))
    a["bo0"] = rep(i["L0_attn_bo"])
    a["wx0"], a["bx0"] = c(i["L0_attn_Wg1"].T), rep(i["L0_attn_bg1"])
    a["wx1"] = c(np.concatenate([i["L0_ffn_gate_w"], i["L0_ffn_dp_w1"]], axis=1))
    a["bx1"] = rep(np.concatenate([i["L0_ffn_gate_b"], i["L0_ffn_dp_b1"]]))
    a["wx3"], a["bx3"] = c(i["L1_ffn_Wg"]), rep(i["L1_ffn_bg"])
    a["dpw2"], a["dpb2"] = rep(i["L0_ffn_dp_w2"]), rep(i["L0_ffn_dp_b2"])
    a["wg2"], a["bg2"], a["g"] = c(i["L0_attn_Wg2"].T), rep(i["L0_attn_bg2"], B), rep(i["L0_attn_g"], B)
    a["w1_0"], a["w2_0"], a["b1_0"], a["b2_0"] = experts(
        i["L0_ffn_ew1"], i["L0_ffn_eb1"], i["L0_ffn_ew2"], i["L0_ffn_eb2"], E0, F0)
    a["w1_1"], a["w2_1"], a["b1_1"], a["b2_1"] = experts(
        i["L1_ffn_W1"], i["L1_ffn_b1"], i["L1_ffn_W2"], i["L1_ffn_b2"], E1, F1)
    return a


def kernel(**inputs):
    import concourse.bacc as bacc
    from concourse.bass_utils import run_bass_kernel_spmd

    nc = bacc.Bacc("TRN2", target_bir_lowering=False, num_devices=1)
    arrays = layout(inputs)
    aps = {n: nc.dram_tensor(f"in_{n}", v.shape, F32, kind="ExternalInput").ap() for n, v in arrays.items()}
    out = nc.dram_tensor("out", (B, T, D), F32, kind="ExternalOutput").ap()
    program(nc, aps, out)
    r = run_bass_kernel_spmd(nc, [{f"in_{n}": v for n, v in arrays.items()}], core_ids=[0])
    return r.results[0]["out"]
```

```python
from contextlib import ExitStack

import concourse.bass as bass
from concourse import mybir

F32 = mybir.dt.float32
F16 = mybir.dt.float16
BF16 = mybir.dt.bfloat16
I32 = mybir.dt.int32
ALU = mybir.AluOpType
ACT = mybir.ActivationFunctionType
AX = mybir.AxisListType

B, T, D = 32, 256, 128
P = 128
TT = T // P
NT = B * TT
H, DH = 16, 8
HG = 4
NJ = H // HG
HID = 64
E0, F0 = 4, 2
E1, F1 = 8, 4
GT = 4
NG = NT // GT
LN_EPS = 1e-5
NORM_EPS = 1e-12
SCALE = DH ** -0.5
NEG = -1e30
MSHIFT = 256.0
WSCALE = 16.0
CH = 8

import math
K_CUTS = [(math.log(math.exp(0.5 + 1.5 * (c - 1.0) / 3.0) - 1.0), op)
          for c, op in ((1.5, ALU.is_ge), (2.5, ALU.is_gt), (3.5, ALU.is_ge))]

SA, CA, GA, SB, CB, GB = range(6)
NX = [HID, E0 + HID, 0, E1]
NMOD = [(0, SA, CA), (0, SB, CB), (1, SA, CA), (1, SB, CB)]


def program(nc, a, out):
    ctx = ExitStack()
    with ctx:
        def sb(name, shape, dt=F32):
            return ctx.enter_context(nc.sbuf_tensor(name, shape, dt))

        def pb(name, shape, dt=F32):
            return ctx.enter_context(nc.psum_tensor(name, shape, dt))

        def sem(name):
            return ctx.enter_context(nc.semaphore(name))

        x_sb = sb("x_sb", [P, NT, D])
        hT = sb("hT", [P, NT * P])
        rows = sb("rows", [P, B, D])
        modT = [sb(f"modT{l}", [P, 6, B]) for l in range(2)]
        wqkv = [sb(f"wqkv{l}", [P, 3 * D]) for l in range(2)]
        wo = [sb(f"wo{l}", [P, D]) for l in range(2)]
        bqkv = sb("bqkv", [P, 3 * D])
        bo = sb("bo", [P, D])
        wx = [sb("wx0", [P, NX[0]]), sb("wx1", [P, NX[1]]), None, sb("wx3", [P, NX[3]])]
        bx = [sb("bx0", [P, NX[0]]), sb("bx1", [P, NX[1]]), None, sb("bx3", [P, NX[3]])]
        dpw2 = sb("dpw2", [P, HID])
        dpb2 = sb("dpb2", [P, 1])
        wg2 = sb("wg2", [HID, H])
        bg2 = sb("bg2", [B, H])
        gst = sb("gst", [B, H])
        shared = sb("shared", [P, 2 * E1 * F1 * P])
        w16 = [sb("w16_0", [P, 2 * E0 * F0 * P])[:].bitcast(F16).rearrange("p (w r n) -> p w r n", w=2, r=2),
               shared[:].bitcast(F16).rearrange("p (w r n) -> p w r n", w=2, r=2)]
        b1 = [sb("b1_0", [P, E0 * F0]), sb("b1_1", [P, E1 * F1])]
        b2 = [sb("b2_0", [P, E0]), sb("b2_1", [P, E1])]
        logit = [sb("logit0", [P, NT, E0]), sb("logit1", [P, NT, E1])]
        comb3 = [sb("comb3_0", [P, NT, 3, E0], BF16), sb("comb3_1", [P, NT, 3, E1], BF16)]
        zdp = sb("zdp", [P, NT, 1])
        gsum = sb("gsum", [HID, B])
        gateB = sb("gateB", [P, B, H])
        ident = sb("ident", [P, P])
        ident16 = sb("ident16", [P, P], F16)
        identb = sb("identb", [P, P], BF16)
        ones = sb("ones", [P, 1])
        spare = sb("spare", [P, CH])
        maskQ = sb("maskQ", [P, P], BF16)
        cT = [sb(f"cT{l}", [P, B]) for l in range(2)]
        ce = [sb(f"ce{l}", [P, B]) for l in range(2)]
        pt = sb("pt", [P, 4, 2, 512])
        free = pt[:].rearrange("p a b c -> p (a b c)")
        wmod = [free[:, l * 6 * D:(l + 1) * 6 * D] for l in range(2)]
        graw, gsign, gmag = [free[0:B, 12 * D + n * 4 * D:12 * D + (n + 1) * 4 * D].rearrange(
            "p (n d) -> p n d", n=4) for n in range(3)]
        gl = sb("gl", [B, H])
        gs = sb("gs", [B, H])
        stats = sb("stats", [P, NT, 6])
        mean = sb("mean", [P, NT])
        rstd = sb("rstd", [P, NT])
        dev = sb("dev", [P, NT])
        var = sb("var", [P, NT])
        z = sb("z", [P, 2, TT, D])
        hcur = sb("hcur", [P, 2, T])
        xt = sb("xt", [P, 2, TT, HID + E0])
        rt = sb("rt", [P, NT, E1])
        rank = sb("rank", [P, NT, E1])
        rm = sb("rm", [P, NT, 1])
        kt = sb("kt", [P, NT, 1])
        ha = sb("ha", [P, T])
        qkv = sb("qkv", [P, 3, TT, D])
        qk = qkv[:, 0:2]
        sq = sb("sq", [P, 2, TT, D])
        n2 = sb("n2", [P, 2 * TT * H, 1])
        rn = sb("rn", [P, 2 * TT * H, 1])
        nt = sb("nt", [P, 2 * TT * H, 1])
        st = sb("st", [P, 2, TT * H, 4, DH], F16)
        qsT = sb("qsT", [P, NJ, T], F16)
        qz = shared[:, 0:HG * NJ * T].bitcast(F16).rearrange("p (b g j t) -> p b g j t", b=2, g=HG, j=NJ)
        ksT = sb("ksT", [P, 2, NJ, T], F16)
        vs = sb("vs", [P, 2, TT, H, 32])
        oT = sb("oT", [P, NJ, T])
        rs = sb("rs", [P, TT * H, 1])
        an = sb("an", [P, TT * H, DH])
        aT = sb("aT", [P, T])
        ao = sb("ao", [P, TT, D])
        mx = sb("mx", [P, TT, NJ, HG])
        GTOK = GT * P
        h16 = hT[:].bitcast(F16).rearrange("p (r n) -> p r n", r=2)
        hid = free.bitcast(F16).rearrange("p (e f r n) -> p e f r n", e=2, f=4, r=2)
        relu = vs[:].rearrange("p a t h c -> p (a t h c)").rearrange("p (k n) -> p k n", k=4)
        crow = oT[:].rearrange("p j t -> p (j t)").rearrange("p (k n) -> p k n", k=2)
        term = ksT[:].rearrange("p a j t -> p (a j t)").bitcast(F32).rearrange("p (k n) -> p k n", k=2)
        acc = st[:].rearrange("p w h r d -> p (w h r d)").bitcast(F32).rearrange("p (k n) -> p k n", k=2)
        xo = sq[:].rearrange("p w t d -> p (w t) d")
        cmp = ksT[:].rearrange("p a j t -> p (a j t)")
        ccur = [sb("ccur0", [P, 2, GT, 3 * E0], BF16), sb("ccur1", [P, 2, GT, 3 * E1], BF16)]
        cT3 = sb("cT3", [3 * E1, 2, GT * P], BF16)
        pick = [sb("pick0", [3 * E0, E0, P], BF16), sb("pick1", [3 * E1, E1, P], BF16)]

        SP = [pb("SP0", [P, 2, 512]), pb("SP1", [P, 2, 512])]
        OP = pb("OP", [P, 2, 512])
        M = pb("M", [P, 2, 512])
        bank = [SP[0][:, 0, :], SP[0][:, 1, :], SP[1][:, 0, :], SP[1][:, 1, :],
                OP[:, 0, :], OP[:, 1, :], M[:, 0, :], M[:, 1, :]]

        g_dram = [nc.dram_tensor(f"g_dram{n}", (B, D), F32, kind="Internal").ap() for n in range(4)]
        gate_dram = nc.dram_tensor("gate_dram", (B, H), F32, kind="Internal").ap()

        phase_end = sem("phase_end")
        w_in, c_in, mod_in = sem("w_in"), sem("c_in"), sem("mod_in")
        x_in = [sem(f"x_in{i}") for i in range(8)]
        row_out, row_in, gate_out, gate_in = sem("row_out"), sem("row_in"), sem("gate_out"), sem("gate_in")
        y_out = sem("y_out")
        idents = sem("idents")
        silu_e, silu_r = sem("silu_e"), sem("silu_r")
        mod_mm, mod_cp, g_mm, g_fin = sem("mod_mm"), sem("mod_cp"), sem("g_mm"), sem("g_fin")
        gl_mm, gl_in, gl_exp, gl_fin = sem("gl_mm"), sem("gl_in"), sem("gl_exp"), sem("gl_fin")

        def sems(kind, n, names):
            return {k: sem(f"{kind}{n}_{k}") for k in names.split()}

        norm_s = [sems("norm", n, "z zT h hT x xin gelu " + ("rexp wload0 wload1 whi wlo" if n % 2 else "gmm gsum")) for n in range(4)]
        att_s = [sems("att", l, "h proj sel qkv stack sT sE mfill mred mrow score exp pv o oT an aT aE wo wr x kE qz guess rn vs")
                 for l in range(2)]
        exp_s = [sems("exp", l, "c cT cE hid relu lo row rowE y term acc turn done") for l in range(2)]

        block = ctx.enter_context(nc.Block())
        ENGINES = 5

        def phase(eng, n):
            eng.drain().then_inc(phase_end, 1)
            eng.wait_ge(phase_end, ENGINES * n)

        LOADS = [(wqkv[0], "wqkv0"), (wqkv[1], "wqkv1"), (wo[0], "wo0"), (wo[1], "wo1"),
                 (bqkv, "bqkv0"), (bo, "bo0"), (wx[0], "wx0"), (wx[1], "wx1"), (wx[3], "wx3"),
                 (bx[0], "bx0"), (bx[1], "bx1"), (bx[3], "bx3"), (dpw2, "dpw2"), (dpb2, "dpb2"),
                 (wg2, "wg2"), (bg2, "bg2"), (gst, "g"), (b1[0], "b1_0"), (b1[1], "b1_1"),
                 (b2[0], "b2_0"), (b2[1], "b2_1")]
        CONDS = [(cT[0], "cT0"), (cT[1], "cT1")]
        MODS = [(wmod[0], "wmod0"), (wmod[1], "wmod1")]
        COLS = [E0 * F0 * P, E1 * F1 * P]
        CHUNKS = 4

        def stage(l, c):
            return free[:, (c % 2) * COLS[l] // 2:(c % 2 + 1) * COLS[l] // 2]

        def weight_part(l, c, part):
            return w16[l][:, c // 2, part, (c % 2) * COLS[l] // 2:(c % 2 + 1) * COLS[l] // 2]

        @block.sync
        def _(sp):
            for dst, name in CONDS:
                sp.dma_start(dst[:, :], a[name]).then_inc(c_in, 16)
            for dst, name in MODS:
                sp.dma_start(dst[:, :], a[name]).then_inc(mod_in, 16)
            xd = a["x"].rearrange("b (t p) d -> p (b t) d", p=P)
            for i in range(8):
                sp.dma_start(x_sb[:, i * 8:i * 8 + 8, :], xd[:, i * 8:i * 8 + 8, :]).then_inc(x_in[i], 16)
            sp.wait_ge(g_fin, 1)
            for n in range(4):
                sp.dma_start(g_dram[n], graw[:, n, :]).then_inc(row_out, 16)

            def spread(n):
                sp.wait_ge(row_out, 64)
                sp.dma_start(rows[:].rearrange("p b d -> p (b d)"),
                             g_dram[n].rearrange("b d -> (b d)").partition_broadcast(P)).then_inc(row_in, 16)

            spread(0)
            sp.wait_ge(gl_fin, 1)
            sp.dma_start(gate_dram, gs[:]).then_inc(gate_out, 16)
            sp.wait_ge(gate_out, 16)
            sp.dma_start(gateB[:].rearrange("p b h -> p (b h)"),
                         gate_dram.rearrange("b h -> (b h)").partition_broadcast(P)).then_inc(gate_in, 16)
            phase(sp, 1)
            phase(sp, 2)
            for n in range(1, 4):
                spread(n)
                if n != 2:
                    l = n // 2
                    for c in range(CHUNKS):
                        if c >= 2:
                            sp.wait_ge(norm_s[n]["wlo"], c - 1)
                        sp.dma_start(stage(l, c), a[f"w{c // 2 + 1}_{l}"][:, (c % 2) * COLS[l] // 2:
                                                                         (c % 2 + 1) * COLS[l] // 2]
                                     ).then_inc(norm_s[n][f"wload{c % 2}"], 16)
                phase(sp, 2 * n + 1)
                if n < 3:
                    phase(sp, 2 * n + 2)
            od = out.rearrange("b (t p) d -> p (b t) d", p=P)
            with sp.Fori(0, NG) as g:
                sp.wait_ge(exp_s[1]["done"], g + 1)
                sp.dma_start(od[:, bass.ts(g, GT), :], x_sb[:, bass.ts(g, GT), :]).then_inc(y_out, 16)
            sp.wait_ge(y_out, 16 * NG)
            phase(sp, 8)

        @block.gpsimd
        def _(pool):
            one_s = ones[:, 0:1].to_broadcast([P, T])
            pool.memset(ident[:], 0.0)
            pool.memset(maskQ[:], 0.0)
            pool.memset(ones[:], 1.0)
            pool.drain()
            pool.affine_select(out=ident[:], in_=ident[:], compare_op=ALU.not_equal, fill=1.0,
                               base=0, pattern=[[-1, P]], channel_multiplier=1)
            pool.affine_select(out=maskQ[:], in_=maskQ[:], compare_op=ALU.is_ge, fill=NEG,
                               base=0, pattern=[[-1, P]], channel_multiplier=1)
            pool.drain()
            pool.tensor_copy(ident16[:], ident[:])
            pool.tensor_copy(identb[:], ident[:])
            pool.drain().then_inc(idents, 1)
            pool.memset(vs[:], 0.0)
            pool.memset(shared[:, 0:HG * NJ * T], 0.0)
            pool.drain()
            pool.memset(vs[:, :, :, :, DH:DH + 1], 1.0)

            def keep(n):
                s = norm_s[n]

                def one(b, par):
                    pool.wait_ge(s["h"], b + 1)
                    if n % 2:
                        pool.tensor_tensor(h16[:, 1, bass.ts(b, T)], hcur[:, par, :], h16[:, 0, bass.ts(b, T)],
                                           ALU.subtract).then_inc(s["hT"], 1)
                    else:
                        pool.tensor_tensor(hT[:, bass.ts(b, T)], hcur[:, par, :], one_s[:, 0:T],
                                           ALU.mult).then_inc(s["hT"], 1)

                with pool.Fori(0, B // 4) as i:
                    for k in range(4):
                        one(4 * i + k, k % 2)

            def weight_low(n):
                s, l = norm_s[n], n // 2
                for c in range(CHUNKS):
                    pool.wait_ge(s["whi"], c + 1)
                    pool.tensor_tensor(weight_part(l, c, 1), stage(l, c), weight_part(l, c, 0),
                                       ALU.subtract).then_inc(s["wlo"], 1)

            def attention(l):
                s = att_s[l]

                def fetch(b, first=False):
                    if not first:
                        pool.wait_ge(s["proj"], 2 * b)
                    pool.tensor_tensor(ha[:], hT[:, bass.ts(b, T)], one_s[:, 0:T], ALU.mult).then_inc(s["h"], 1)

                def newton(b):
                    pool.wait_ge(s["guess"], b + 1)
                    for k in range(3):
                        pool.tensor_tensor(nt[:], rn[:], rn[:], ALU.mult)
                        pool.drain()
                        pool.tensor_tensor(nt[:], nt[:], n2[:], ALU.mult)
                        pool.drain()
                        pool.tensor_scalar(nt[:], nt[:], -0.5, 1.5, ALU.mult, ALU.add)
                        pool.drain()
                        last = pool.tensor_tensor(rn[:], rn[:], nt[:], ALU.mult)
                        if k < 2:
                            pool.drain()
                    last.then_inc(s["rn"], 1)

                def place_v(b, par, first=False):
                    pool.wait_ge(s["qkv"], b + 1)
                    if not first:
                        pool.wait_ge(s["pv"], CH * (b - 1))
                    v = qkv[:, 2].rearrange("p t (h d) -> p (t h) d", d=DH)
                    pool.tensor_tensor(vs[:, par, :, :, 0:DH].rearrange("p t h d -> p (t h) d"), v, one_s[:, 0:T].rearrange("p (n d) -> p n d", d=DH),
                                       ALU.mult).then_inc(s["vs"], 1)

                def select(b, u):
                    pool.wait_ge(s["exp"], CH * b + u + 1)
                    pool.tensor_tensor(spare[:, u:u + 1], ones[:], ones[:], ALU.mult)
                    for i in range(2):
                        diag = pt[:, u % 4, i, :].rearrange("p (k q) -> p k q", k=2)[:, :, 0:P]
                        last = pool.affine_select(out=diag, in_=diag, compare_op=ALU.is_ge, fill=0.0, base=0,
                                                  pattern=[[0, 2], [1, P]], channel_multiplier=-1)
                    last.then_inc(s["sel"], 1)

                def one(b, par, first=False, ahead=3):
                    if l:
                        pool.drain()
                        select(b, 0)
                    if ahead >= 1:
                        place_v(b + 1, 1 - par, first)
                    if l:
                        for u in range(1, CH):
                            select(b, u)
                    if ahead >= 3:
                        fetch(b + 3)
                    if l == 0 and ahead >= 2:
                        newton(b + 2)

                fetch(0, True)
                fetch(1)
                if l == 0:
                    newton(0)
                place_v(0, 0, True)
                fetch(2)
                if l == 0:
                    newton(1)
                one(0, 0, True)
                one(1, 1)
                with pool.Fori(1, B // 2 - 2) as i:
                    for par in range(2):
                        one(2 * i + par, par)
                one(B - 4, 0)
                one(B - 3, 1, ahead=2)
                one(B - 2, 0, ahead=1)
                one(B - 1, 1, ahead=0)

            def experts(l, E):
                s = exp_s[l]

                def current(g, par, first=False):
                    if not first:
                        pool.wait_ge(s["cT"], g - 1)
                    pool.tensor_copy(ccur[l][:, par],
                                     comb3[l][:, bass.ts(g, GT)].rearrange("p t r e -> p t (r e)")).then_inc(s["c"], 1)

                def one(g, par, nxt=True, first=False):
                    if nxt:
                        current(g + 1, 1 - par, first)
                    for e in range(1, E):
                        pool.wait_ge(s["term"], E * g + e + 1)
                        pool.tensor_tensor(acc[:, par, :], acc[:, par, :], term[:, e % 2, :],
                                           ALU.add).then_inc(s["acc"], 1)
                        if e + 1 < E:
                            pool.drain()

                current(0, 0, True)
                one(0, 0, first=True)
                one(1, 1)
                with pool.Fori(1, NG // 2 - 1) as i:
                    for par in range(2):
                        one(2 * i + par, par)
                one(NG - 2, 0)
                one(NG - 1, 1, nxt=False)

            keep(0)
            phase(pool, 1)
            attention(0)
            phase(pool, 2)
            keep(1)
            weight_low(1)
            phase(pool, 3)
            experts(0, E0)
            phase(pool, 4)
            keep(2)
            pool.memset(st[:], 0.0)
            pool.memset(vs[:], 0.0)
            pool.drain()
            pool.memset(vs[:, :, :, :, DH:DH + 1], 1.0)
            pool.memset(st[:, 1, :, 3, 0:1], MSHIFT)
            phase(pool, 5)
            attention(1)
            phase(pool, 6)
            keep(3)
            weight_low(3)
            phase(pool, 7)
            experts(1, E1)
            phase(pool, 8)

        @block.scalar
        def _(act):
            act.wait_ge(c_in, 16 * len(CONDS))
            for l in range(2):
                act.activation(ce[l][:], cT[l][:], ACT.Exp, scale=-1.0).then_inc(silu_e, 1)
            for dst, name in LOADS:
                act.dma_start(dst[:], a[name]).then_inc(w_in, 16)
            act.wait_ge(w_in, 16 * len(LOADS))

            def norm(n):
                s, (l, sh, sc) = norm_s[n], NMOD[n]

                def mod(b, par, first=False):
                    act.wait_ge(s["zT"], b + 1)
                    if not first:
                        act.wait_ge(s["hT"], b - 1)
                        if NX[n]:
                            act.wait_ge(s["x"], b - 1)
                    for dst in [h16[:, 0, bass.ts(b, T)]] * (n % 2) + [hcur[:, par, :]]:
                        last = act.activation(dst, bank[par][:, 0:T], ACT.Identity,
                                              bias=modT[l][:, sh, bass.ds(b, 1)],
                                              scale=modT[l][:, sc, bass.ds(b, 1)])
                    last.then_inc(s["h"], 1)

                def gelu(b, par):
                    act.wait_ge(s["xin"], b + 1)
                    act.activation(xt[:, par, :, 0:HID], xt[:, par, :, 0:HID], ACT.Gelu).then_inc(s["gelu"], 1)

                def one(b, par, first=False):
                    mod(b, par, first)
                    if n == 0 and not first:
                        gelu(b - 2, par)

                for b in range(4):
                    one(b, b % 2, b < 2)
                with act.Fori(1, B // 4) as i:
                    for k in range(4):
                        one(4 * i + k, k % 2)
                if n == 0:
                    gelu(B - 2, 0)
                    gelu(B - 1, 1)

            act.wait_ge(mod_cp, 2)
            norm(0)
            act.wait_ge(gl_in, 1)
            act.activation(gl[:], gl[:], ACT.Exp, scale=-1.0)
            act.activation(gs[:], gst[:], ACT.Exp, scale=-1.0)
            act.drain().then_inc(gl_exp, 1)
            phase(act, 1)

            def attention(l):
                s = att_s[l]
                W = 512 if l == 0 else 384

                def prep(b, par, first=False, which=(0, 1)):
                    n = 3 if l else 2
                    if not first:
                        act.wait_ge(s["qz"], 2 * b)
                    for i, dst in enumerate([qsT[:], ksT[:, par]]):
                        if i not in which or (l and i):
                            continue
                        act.wait_ge(s["sT"], n * b + i + 1)
                        act.activation(dst.rearrange("p j t -> p (j t)"),
                                       M[:, i, :].bitcast(F16), ACT.Copy).then_inc(s["sE"], 1)

                def prep_again(b, par):
                    if l:
                        act.wait_ge(s["sT"], 3 * b + 3)
                        for half in range(2):
                            cols = slice(half * 512, half * 512 + 512)
                            act.activation(qsT[:].rearrange("p j t -> p (j t)")[:, cols],
                                           M[:, 0, :].bitcast(F16)[:, cols], ACT.Copy).then_inc(s["sE"], 1)

                def tail_o(b, i, first=False):
                    act.wait_ge(s["pv"], CH * b + 4 * i + 4)
                    if i == 0 and not first:
                        act.wait_ge(s["oT"], 2 * b)
                    act.activation(oT[:].rearrange("p j t -> p (j t)")[:, i * 512:i * 512 + 512],
                                   OP[:, i, :], ACT.Copy).then_inc(s["o"], 1)

                def tail_a(b):
                    act.wait_ge(s["aT"], b + 1)
                    act.activation(aT[:], OP[:, 1, 0:T], ACT.Copy).then_inc(s["aE"], 1)

                def exp(b, u, first=False):
                    act.wait_ge(s["score"], CH * b + u + 1)
                    if not (first and u < 4):
                        act.wait_ge(s["pv"], CH * b + u - 3)
                    act.activation(pt[:, u % 4, :, 0:W], SP[u % 2][:, :, 0:W], ACT.Exp,
                                   scale=SCALE).then_inc(s["exp"], 1)

                def one(b, par, first=False, tail=True, nxt=True):
                    for u in range(CH):
                        exp(b, u, first)
                        if l == 0 and u == 0 and tail:
                            tail_o(b - 1, 1)
                        if u == (3 if l else 4) and tail:
                            tail_a(b - 1)
                        if l and u == 1 and nxt:
                            prep(b + 1, 1 - par)
                        if u == (6 if l else 5):
                            tail_o(b, 0, first)
                        if l == 0 and u in (5, 6) and nxt:
                            prep(b + 1, 1 - par, which=(u - 5,))
                    if nxt:
                        prep_again(b + 1, 1 - par)
                    if l:
                        tail_o(b, 1)

                prep(0, 0, True)
                prep_again(0, 0)
                one(0, 0, True, tail=False)
                one(1, 1)
                with act.Fori(1, B // 2 - 1) as i:
                    for par in range(2):
                        one(2 * i + par, par)
                one(B - 2, 0)
                one(B - 1, 1, nxt=False)
                if l == 0:
                    tail_o(B - 1, 1)
                tail_a(B - 1)

            def weight_high(n, c):
                s, l = norm_s[n], n // 2
                act.wait_ge(s[f"wload{c % 2}"], 16 * (c // 2 + 1))
                act.activation(weight_part(l, c, 0), stage(l, c), ACT.Copy, scale=WSCALE)
                act.drain()
                act.activation(stage(l, c), stage(l, c), ACT.Copy, scale=WSCALE).then_inc(s["whi"], 1)

            def router(n):
                s, E = norm_s[n], (E0, E1)[n // 2]
                for c in range(CHUNKS - 1):
                    weight_high(n, c)
                act.wait_ge(s["rexp"], 1)
                act.activation(rt[:, :, 0:E], rt[:, :, 0:E], ACT.Exp).then_inc(s["gelu"], 1)
                weight_high(n, CHUNKS - 1)

            def experts(l, E, F):
                s = exp_s[l]

                def one(g, par, first=False):
                    for e in range(E):
                        for f in range(F):
                            k = e * F + f
                            act.wait_ge(s["hid"], E * F * g + k + 1)
                            if f == 0 and not (first and par == 0 and e < 2):
                                act.wait_ge(s["y"], E * g + e - 1)
                            if not (first and par == 0 and k < 4):
                                act.wait_ge(s["lo"], E * F * g + k - 3)
                            act.activation(hid[:, e % 2, f, 0, :], bank[k % 4], ACT.Relu,
                                           bias=b1[l][:, k:k + 1], scale=1.0 / WSCALE)
                            act.activation(relu[:, k % 4, :], bank[k % 4], ACT.Relu,
                                           bias=b1[l][:, k:k + 1], scale=1.0 / WSCALE).then_inc(s["relu"], 1)
                        act.wait_ge(s["row"], E * g + e + 1)
                        if not (first and par == 0 and e < 2):
                            act.wait_ge(s["term"], E * g + e - 1)
                        act.activation(crow[:, e % 2, :], bank[6], ACT.Copy).then_inc(s["rowE"], 1)

                one(0, 0, True)
                one(1, 1, True)
                with act.Fori(1, NG // 2) as i:
                    for par in range(2):
                        one(2 * i + par, par)

            attention(0)
            phase(act, 2)
            norm(1)
            router(1)
            phase(act, 3)
            experts(0, E0, F0)
            phase(act, 4)
            norm(2)
            phase(act, 5)
            attention(1)
            phase(act, 6)
            norm(3)
            router(3)
            phase(act, 7)
            experts(1, E1, F1)
            phase(act, 8)

        @block.vector
        def _(dve):
            def first_stats(chunks):
                for i in chunks:
                    dve.wait_ge(x_in[i], 16)
                    for k in range(8):
                        dve.bn_stats(stats[:, 8 * i + k, :], x_sb[:, 8 * i + k, :])

            dve.wait_ge(silu_e, 2)
            for l in range(2):
                dve.tensor_scalar(ce[l][:], ce[l][:], 1.0, None, ALU.add)
            dve.drain()
            for l in range(2):
                dve.reciprocal(ce[l][:], ce[l][:])
            dve.drain()
            for l in range(2):
                dve.tensor_tensor(ce[l][:], ce[l][:], cT[l][:], ALU.mult).then_inc(silu_r, 1)
            first_stats(range(3))
            for l in range(2):
                dve.wait_ge(mod_mm, l + 1)
                dve.tensor_copy(modT[l][:].rearrange("p m b -> p (m b)"), bank[l][:, 0:6 * B])
            dve.drain()
            for l in range(2):
                dve.tensor_scalar(modT[l][:, CA, :], modT[l][:, CA, :], 1.0, None, ALU.add)
                dve.tensor_scalar(modT[l][:, CB, :], modT[l][:, CB, :], 1.0, None, ALU.add).then_inc(mod_cp, 1)
            dve.wait_ge(g_mm, 1)
            dve.tensor_copy(graw.rearrange("p n d -> p (n d)"), bank[2][0:B, :])
            dve.drain()
            flat = [v.rearrange("p n d -> p (n d)") for v in (graw, gsign, gmag)]
            dve.tensor_scalar(flat[1], flat[0], 0.0, 2.0, ALU.is_ge, ALU.mult)
            dve.scalar_tensor_tensor(flat[2], flat[0], -1.0, flat[0], ALU.mult, ALU.max)
            dve.drain()
            dve.tensor_scalar(flat[2], flat[2], 0.25, None, ALU.max)
            dve.drain()
            dve.scalar_tensor_tensor(flat[0], flat[1], -1.0, flat[2], ALU.add, ALU.mult).then_inc(g_fin, 1)

            def guess(y, x):
                yi = y.bitcast(I32)
                dve.tensor_scalar(yi, x.bitcast(I32), 1, None, ALU.logical_shift_right)
                dve.drain()
                return dve.tensor_scalar(yi, yi, -1.0, float(0x5F3759DF), ALU.mult, ALU.add)

            def rsqrt(y, x, t):
                guess(y, x)
                for _ in range(3):
                    dve.drain()
                    dve.tensor_tensor(t, y, y, ALU.mult)
                    dve.drain()
                    dve.scalar_tensor_tensor(t, t, -0.5, x, ALU.mult, ALU.mult)
                    dve.drain()
                    dve.scalar_tensor_tensor(y, t, 1.5, y, ALU.add, ALU.mult)
                dve.drain()

            def norm(n):
                s = norm_s[n]

                if n == 0:
                    first_stats(range(3, 8))
                dve.drain()
                dve.tensor_tensor(mean[:], stats[:, :, 1], stats[:, :, 4], ALU.add)
                dve.tensor_tensor(dev[:], stats[:, :, 1], stats[:, :, 4], ALU.subtract)
                dve.tensor_tensor(var[:], stats[:, :, 2], stats[:, :, 5], ALU.add)
                dve.drain()
                dve.tensor_scalar(mean[:], mean[:], 0.5, None, ALU.mult)
                dve.tensor_tensor(dev[:], dev[:], dev[:], ALU.mult)
                dve.tensor_scalar(var[:], var[:], 1.0 / D, LN_EPS, ALU.mult, ALU.add)
                dve.drain()
                dve.scalar_tensor_tensor(var[:], dev[:], 0.25, var[:], ALU.mult, ALU.add)
                dve.drain()
                rsqrt(rstd[:], var[:], dev[:])

                def ln(b, par, first=False):
                    if not first:
                        dve.wait_ge(s["zT"], b - 1)
                    for t in range(TT):
                        k = bass.ds(2 * b + t, 1)
                        dve.tensor_scalar(z[:, par, t, :], x_sb[:, 2 * b + t, :], mean[:, k],
                                          rstd[:, k], ALU.subtract, ALU.mult).then_inc(s["z"], 1)

                def extra(b, par):
                    if n == 2:
                        return
                    dve.wait_ge(s["x"], b + 1)
                    nx = NX[n]
                    src = bank[2 + par][:, 0:TT * nx].rearrange("p (t x) -> p t x", t=TT)
                    bias = bx[n][:].unsqueeze(1).to_broadcast([P, TT, nx])
                    if n == 3:
                        dve.tensor_tensor(logit[1][:, bass.ts(b, TT), :], src, bias, ALU.add).then_inc(s["xin"], 1)
                        return
                    dve.tensor_tensor(xt[:, par, :, 0:nx], src, bias, ALU.add).then_inc(s["xin"], 1)
                    if n == 0:
                        return
                    dve.drain()
                    dve.tensor_copy(logit[0][:, bass.ts(b, TT), :], xt[:, par, :, 0:E0])
                    for t in range(TT):
                        dve.scalar_tensor_tensor(xt[:, par, t, E0:nx], xt[:, par, t, E0:nx], 0.0, dpw2[:],
                                                 ALU.max, ALU.mult, accum_out=zdp[:, 2 * b + t, :])
                    dve.drain()

                def sums(b, par):
                    if n == 0:
                        dve.wait_ge(s["gmm"], b + 1)
                        dve.tensor_copy(gsum[:, bass.ds(b, 1)], bank[4 + par][0:HID, 0:1]).then_inc(s["gsum"], 1)

                def one(b, par, lag=4):
                    ln(b, par, lag < 2)
                    if lag == 4:
                        sums(b - 4, par)
                    if lag >= 2:
                        extra(b - 2, par)

                for b in range(4):
                    one(b, b % 2, b // 2 * 2)
                with dve.Fori(1, B // 4) as i:
                    for k in range(4):
                        one(4 * i + k, k % 2)
                for par in range(2):
                    sums(B - 4 + par, par)
                    extra(B - 2 + par, par)
                for par in range(2):
                    sums(B - 2 + par, par)

            def tile_stats(k, tiles):
                for t in range(tiles):
                    dve.bn_stats(stats[:, k + t, :], x_sb[:, k + t, :])

            norm(0)
            dve.wait_ge(gl_mm, 1)
            dve.scalar_tensor_tensor(gl[:], bank[6][0:B, 0:H], 1.0 / T, bg2[:], ALU.mult, ALU.add).then_inc(gl_in, 1)
            dve.wait_ge(gl_exp, 1)
            dve.tensor_scalar(gl[:], gl[:], 1.0, None, ALU.add)
            dve.drain()
            dve.scalar_tensor_tensor(gs[:], gs[:], 1.0, gl[:], ALU.add, ALU.mult)
            dve.drain()
            dve.reciprocal(gs[:], gs[:]).then_inc(gl_fin, 1)
            dve.wait_ge(gate_in, 16)
            dve.wait_ge(row_in, 16)
            phase(dve, 1)

            def attention(l):
                s = att_s[l]

                def prep_qkv(b, first=False):
                    if not first:
                        dve.wait_ge(s["vs"], b)
                        dve.wait_ge(s["stack"], 2 * b)
                    for t in range(TT):
                        dve.wait_ge(s["proj"], 2 * b + t + 1)
                        dve.tensor_tensor(qkv[:, :, t, :], M[:, t, 0:3 * D].rearrange("p (w d) -> p w d", w=3),
                                          bqkv[:].rearrange("p (w d) -> p w d", w=3), ALU.add)
                    dve.drain().then_inc(s["qkv"], 1)
                    if l == 0:
                        flat = qk.rearrange("p w t d -> p (w t d)")
                        dve.tensor_tensor(sq[:].rearrange("p w t d -> p (w t d)"), flat, flat, ALU.mult)
                        dve.drain()
                        dve.tensor_reduce(n2[:], sq[:].rearrange("p w t (h d) -> p (w t h) d", d=DH), AX.X, ALU.add)
                        dve.drain()
                        dve.tensor_scalar(n2[:], n2[:], NORM_EPS ** 2, None, ALU.max)
                        dve.drain()
                        guess(rn[:, :, 0], n2[:, :, 0]).then_inc(s["guess"], 1)

                def split_tile(b, t, first=False):
                    dve.wait_ge(s["proj"], 2 * b + t + 1)
                    if not first:
                        dve.wait_ge(s["sT"], 3 * b)
                        dve.wait_ge(s["vs"], b)
                    q, k = [M[:, 1 - t, w * D:(w + 1) * D].rearrange("p (h d) -> p h d", d=DH) for w in range(2)]
                    sq_, sk = [st[:, w, t * H:(t + 1) * H] for w in range(2)]
                    wide = [P, H, 2, DH]
                    dve.tensor_copy(sq_[:, :, 0:3:2, :], q.unsqueeze(2).to_broadcast(wide))
                    dve.tensor_copy(sk[:, :, 0:2, :], k.unsqueeze(2).to_broadcast(wide))
                    dve.tensor_copy(qkv[:, 2, t, :], M[:, 1 - t, 2 * D:3 * D])
                    dve.drain()
                    dve.tensor_tensor(sq_[:, :, 1, :], q, sq_[:, :, 0, :], ALU.subtract)
                    dve.tensor_tensor(sk[:, :, 2, :], k, sk[:, :, 0, :], ALU.subtract)
                    if t:
                        dve.drain().then_inc(s["qkv"], 1)

                def prep_split(b, first=False):
                    heads = qk.rearrange("p w t (h d) -> p (w t h) d", d=DH)
                    dve.wait_ge(s["rn"], b + 1)
                    dve.tensor_tensor(heads, heads, rn[:].to_broadcast([P, 2 * TT * H, DH]), ALU.mult)
                    dve.drain()
                    if not first:
                        dve.wait_ge(s["sT"], 2 * b)
                    wide = [P, TT * H, 2, DH]
                    for w in range(2):
                        src = heads[:, w * TT * H:(w + 1) * TT * H, :]
                        hi = st[:, 0, :, 0:3:2, :] if w == 0 else st[:, 1, :, 0:2, :]
                        dve.tensor_copy(hi, src.unsqueeze(2).to_broadcast(wide))
                    dve.drain()
                    for w in range(2):
                        src = heads[:, w * TT * H:(w + 1) * TT * H, :]
                        lo = st[:, 0, :, 1:4:2, :] if w == 0 else st[:, 1, :, 2:4, :]
                        dve.tensor_tensor(lo, src.unsqueeze(2).to_broadcast(wide),
                                          st[:, w, :, 0:1, :].to_broadcast(wide), ALU.subtract).then_inc(s["stack"], 1)

                def prep_keys(b, par):
                    dve.wait_ge(s["sT"], 3 * b + 2)
                    dve.tensor_copy(ksT[:, par].rearrange("p j t -> p (j t)"),
                                    M[:, 1, :].bitcast(F16)).then_inc(s["kE"], 1)

                def prep_max(b, k):
                    dve.wait_ge(s["mfill"], 12 * b + k + 1)
                    jj, g = k // 4, k % 4
                    to = mx[:, 1, 2 * jj:2 * jj + 2, g:g + 1] if k < 8 else mx[:, 0, :, g:g + 1]
                    dve.tensor_reduce(to, M[:, k % 2, :].rearrange("p (j k) -> p j k", j=2 if k < 8 else 4),
                                      AX.X, ALU.max).then_inc(s["mred"], 1)

                def prep_row(b):
                    dve.drain()
                    dve.tensor_scalar(st[:, 0, :, 3, 0:1], mx[:].rearrange("p t j g -> p (t j g)").unsqueeze(2),
                                      -1.0 / MSHIFT, None, ALU.mult).then_inc(s["mrow"], 1)

                def prep_heads(b, par, half, first=False):
                    dve.wait_ge(s["sE"], 3 * b + 2 + half if l else 2 * b + 1)
                    if not first:
                        dve.wait_ge(s["score"], CH * (b - 1))
                    heads, js = (range(HG), slice(2 * half, 2 * half + 2)) if l else ((2 * half, 2 * half + 1), slice(NJ))
                    for g in heads:
                        rows32 = slice(32 * g, 32 * g + 32)
                        last = dve.tensor_copy(qz[rows32, par, g, js], qsT[rows32, js])
                    last.then_inc(s["qz"], 1)

                def tail_n(b, t):
                    dve.wait_ge(s["oT"], 2 * b + t + 1)
                    o = OP[:, 1].rearrange("p (h c) -> p h c", c=32)
                    r = rs[:, t * H:(t + 1) * H, :]
                    dve.reciprocal(r, o[:, :, DH:DH + 1])
                    dve.drain()
                    if l == 0:
                        dve.tensor_tensor(r.rearrange("p h o -> p o h"), r.rearrange("p h o -> p o h"),
                                          gateB[:, bass.ds(b, 1), :], ALU.mult)
                        dve.drain()
                    dve.tensor_tensor(an[:, t * H:(t + 1) * H, :], o[:, :, 0:DH], r.to_broadcast([P, H, DH]),
                                      ALU.mult).then_inc(s["an"], 1)

                def tail_x(b, first=False):
                    dve.wait_ge(s["wo"], b + 1)
                    w = OP[:, 1, T:T + TT * D].rearrange("p (t d) -> p t d", t=TT)
                    ga = rows[:, bass.ds(b, 1), :].to_broadcast([P, TT, D])
                    if l == 0 and not first:
                        tile_stats(TT * (b - 1), TT)
                    if l == 0:
                        dve.tensor_tensor(ao[:], w, bo[:].unsqueeze(1).to_broadcast([P, TT, D]),
                                          ALU.add).then_inc(s["wr"], 1)
                        dve.drain()
                        dve.tensor_tensor(ao[:], ao[:], ga, ALU.mult)
                    else:
                        dve.tensor_tensor(ao[:], w, ga, ALU.mult).then_inc(s["wr"], 1)
                    dve.drain()
                    xs = x_sb[:, bass.ts(b, TT), :]
                    dve.tensor_tensor(xs, xs, ao[:], ALU.add).then_inc(s["x"], 1)

                def one(b, par, tail=True, nxt=True, nxt2=True, first=False, second=False):
                    if l == 0:
                        if nxt:
                            prep_split(b + 1)
                        if tail:
                            tail_n(b - 1, 0)
                            tail_n(b - 1, 1)
                        if nxt2:
                            prep_qkv(b + 2)
                        if tail:
                            tail_x(b - 1, second)
                    else:
                        if nxt:
                            prep_keys(b + 1, 1 - par)
                        for k in range(12):
                            if k in (0, 2) and tail:
                                tail_n(b - 1, k // 2)
                            if k == 7 and tail:
                                tail_x(b - 1, second)
                            if nxt:
                                prep_max(b + 1, k)
                        if nxt:
                            prep_row(b + 1)
                        if tail:
                            if not nxt:
                                dve.drain()
                            tile_stats(TT * (b - 1), TT)
                    if l and nxt2:
                        split_tile(b + 2, 0)
                    if nxt:
                        prep_heads(b + 1, 1 - par, 0, first)
                    if l and nxt2:
                        split_tile(b + 2, 1)
                    if nxt:
                        prep_heads(b + 1, 1 - par, 1, first)

                if l:
                    split_tile(0, 0, True)
                    split_tile(0, 1, True)
                    prep_keys(0, 0)
                    for k in range(12):
                        prep_max(0, k)
                    prep_row(0)
                    split_tile(1, 0)
                    split_tile(1, 1)
                else:
                    prep_qkv(0, True)
                    prep_split(0, True)
                    prep_qkv(1)
                for half in range(2):
                    prep_heads(0, 0, half, True)
                one(0, 0, tail=False, first=True)
                one(1, 1, second=True)
                with dve.Fori(1, B // 2 - 1) as i:
                    for par in range(2):
                        one(2 * i + par, par)
                one(B - 2, 0, nxt2=False)
                one(B - 1, 1, nxt=False, nxt2=False)
                tail_n(B - 1, 0)
                tail_n(B - 1, 1)
                tail_x(B - 1)
                dve.drain()
                tile_stats(NT - TT, TT)

            def route(n, l, E):
                s = norm_s[n]
                dve.drain()
                if l == 0:
                    for k, (cut, op) in enumerate(K_CUTS):
                        dst = kt if k == 0 else rm
                        dve.tensor_scalar(dst[:], zdp[:], dpb2[:, 0:1], cut, ALU.add, op)
                        dve.drain()
                        if k:
                            dve.tensor_tensor(kt[:], kt[:], rm[:], ALU.add)
                            dve.drain()
                    dve.tensor_scalar(kt[:], kt[:], 1.0, None, ALU.add)
                L = logit[l]
                dve.tensor_reduce(rm[:], L[:], AX.X, ALU.max)
                beats, at = [], 0
                for o in range(E - 1):
                    n_after = E - 1 - o
                    beats.append(cmp[:, at:at + NT * n_after].rearrange("p (n e) -> p n e", e=n_after))
                    at += NT * n_after
                    dve.tensor_tensor(beats[o], L[:, :, o:o + 1].to_broadcast([P, NT, n_after]),
                                      L[:, :, o + 1:E], ALU.is_ge)
                for e in range(E):
                    dve.memset(rank[:, :, e:e + 1], float(E - 1 - e))
                dve.memset(rt[:, :, E - 1:E], 0.0)
                dve.drain()
                for o in range(E - 1):
                    dve.tensor_reduce(rt[:, :, o:o + 1], beats[o], AX.X, ALU.add)
                    dve.tensor_tensor(rank[:, :, o + 1:E], rank[:, :, o + 1:E], beats[o], ALU.add)
                    dve.drain()
                dve.tensor_tensor(rank[:, :, 0:E], rank[:, :, 0:E], rt[:, :, 0:E], ALU.subtract)
                dve.drain()
                kept = kt[:].to_broadcast([P, NT, E]) if l == 0 else None
                if l == 0:
                    dve.tensor_tensor(rank[:, :, 0:E], rank[:, :, 0:E], kept, ALU.is_lt)
                else:
                    dve.tensor_scalar(rank[:, :, 0:E], rank[:, :, 0:E], 2.0, None, ALU.is_lt)
                dve.tensor_tensor(rt[:, :, 0:E], L[:], rm[:].to_broadcast([P, NT, E]), ALU.subtract)
                dve.drain().then_inc(s["rexp"], 1)
                dve.wait_ge(s["gelu"], 1)
                dve.tensor_tensor(rt[:, :, 0:E], rt[:, :, 0:E], rank[:, :, 0:E], ALU.mult)
                dve.drain()
                dve.tensor_reduce(rm[:], rt[:, :, 0:E], AX.X, ALU.add)
                dve.drain()
                dve.reciprocal(rm[:], rm[:])
                dve.drain()
                dve.tensor_tensor(rt[:, :, 0:E], rt[:, :, 0:E], rm[:].to_broadcast([P, NT, E]), ALU.mult)
                for part in range(3):
                    dve.drain()
                    dve.tensor_copy(comb3[l][:, :, part, :], rt[:, :, 0:E])
                    if part < 2:
                        dve.drain()
                        dve.tensor_tensor(rt[:, :, 0:E], rt[:, :, 0:E], comb3[l][:, :, part, :], ALU.subtract)
                each = slice(0, 3 * E)
                pk = rank[each, 0, 0:E]
                dve.tensor_tensor(pk, ident[each, 0:E], ident[each, E:2 * E], ALU.add)
                dve.drain()
                dve.tensor_tensor(pk, pk, ident[each, 2 * E:3 * E], ALU.add)
                dve.tensor_scalar(b2[l][:], b2[l][:], WSCALE, None, ALU.mult)
                dve.drain()
                dve.tensor_copy(pick[l][:], pk.unsqueeze(2).to_broadcast([3 * E, E, P]))

            def experts(l, E, F):
                s = exp_s[l]

                def weights(g, par):
                    dve.wait_ge(s["cT"], g + 1)
                    dve.tensor_copy(cT3[0:3 * E, par, :],
                                    bank[7][0:3 * E, 0:GTOK // 2].bitcast(BF16)).then_inc(s["cE"], 1)

                def low(g, e):
                    for f in range(F):
                        k = e * F + f
                        dve.wait_ge(s["relu"], E * F * g + k + 1)
                        dve.tensor_tensor(hid[:, e % 2, f, 1, :], relu[:, k % 4, :], hid[:, e % 2, f, 0, :],
                                          ALU.subtract).then_inc(s["lo"], 1)

                def weigh(g, par, e, first=False, head=False):
                    dve.wait_ge(s["y"], E * g + e + 1)
                    dve.wait_ge(s["rowE"], E * g + e + 1)
                    if e == 0:
                        if not first:
                            dve.wait_ge(s["turn"], g - 1)
                        to = acc[:, par, :]
                    else:
                        if e > 2:
                            dve.wait_ge(s["acc"], (E - 1) * g + e - 2)
                        elif not head:
                            dve.wait_ge(s["acc"], (E - 1) * g)
                        to = term[:, e % 2, :]
                    dve.scalar_tensor_tensor(to, bank[4 + e % 2], b2[l][:, e:e + 1], crow[:, e % 2, :],
                                             ALU.add, ALU.mult).then_inc(s["term"], 1)

                def finish(g, first=False):
                    if l == 0 and not first:
                        tile_stats(GT * (g - 1), GT)
                    dve.wait_ge(s["turn"], g + 1)
                    for k in range(2):
                        v = bank[7].rearrange("p (t d) -> p t d", d=D)[:, 2 * k:2 * k + 2, :]
                        dve.scalar_tensor_tensor(xo[:, 2 * k:2 * k + 2, :], v, 1.0 / WSCALE,
                                                 rows[:, bass.ds(2 * g + k, 1), :].to_broadcast([P, TT, D]),
                                                 ALU.mult, ALU.mult)
                    dve.drain()
                    xs = x_sb[:, bass.ts(g, GT), :]
                    dve.tensor_tensor(xs, xs, xo, ALU.add).then_inc(s["done"], 1)

                def one(g, par, prev=True, nxt=True, first=False):
                    for e in range(E):
                        low(g, e)
                        if e:
                            weigh(g, par, e - 1, first, not prev)
                        elif prev:
                            weigh(g - 1, 1 - par, E - 1)
                        if e == 1 and nxt:
                            weights(g + 1, 1 - par)
                        if e == 2 and prev:
                            finish(g - 1, first)

                weights(0, 0)
                one(0, 0, prev=False, first=True)
                one(1, 1, first=True)
                with dve.Fori(1, NG // 2 - 1) as i:
                    for par in range(2):
                        one(2 * i + par, par)
                one(NG - 2, 0)
                one(NG - 1, 1, nxt=False)
                weigh(NG - 1, 1, E - 1)
                finish(NG - 1)
                if l == 0:
                    dve.drain()
                    tile_stats(NT - GT, GT)

            attention(0)
            phase(dve, 2)
            norm(1)
            route(1, 0, E0)
            dve.wait_ge(row_in, 32)
            phase(dve, 3)
            experts(0, E0, F0)
            phase(dve, 4)
            norm(2)
            dve.wait_ge(row_in, 48)
            phase(dve, 5)
            attention(1)
            phase(dve, 6)
            norm(3)
            route(3, 1, E1)
            dve.wait_ge(row_in, 64)
            phase(dve, 7)
            experts(1, E1, F1)
            phase(dve, 8)

        @block.tensor
        def _(pe):
            pe.wait_ge(idents, 1)
            pe.wait_ge(mod_in, 16 * len(MODS))
            for l in range(2):
                pe.wait_ge(silu_r, l + 1)
                for m in range(6):
                    last = pe.matmul(bank[l][:, m * B:(m + 1) * B], wmod[l][:, m * D:(m + 1) * D], ce[l][:],
                                     start=True, stop=True)
                last.then_inc(mod_mm, 1)
            for n in range(4):
                l, m = n // 2, (GA, GB)[n % 2]
                last = pe.matmul(bank[2][0:B, n * D:(n + 1) * D], ce[l][:], wmod[l][:, m * D:(m + 1) * D],
                                 start=True, stop=True)
            last.then_inc(g_mm, 1)
            pe.wait_ge(mod_cp, 2)
            pe.wait_ge(g_fin, 1)
            pe.wait_ge(w_in, 16 * len(LOADS))

            def norm(n):
                s = norm_s[n]

                def turn(b, par, first=False):
                    if not first:
                        pe.wait_ge(s["h"], b - 1)
                    for t in range(TT):
                        pe.wait_ge(s["z"], TT * b + t + 1)
                        last = pe.transpose(bank[par][:, t * P:(t + 1) * P], z[:, par, t, :], ident[:])
                    last.then_inc(s["zT"], 1)

                def project(b, par, first=False):
                    if not NX[n]:
                        return
                    pe.wait_ge(s["h"], b + 1)
                    if not first:
                        pe.wait_ge(s["xin"], b - 1)
                    for t in range(TT):
                        last = pe.matmul(bank[2 + par][:, t * NX[n]:(t + 1) * NX[n]],
                                         hcur[:, par, t * P:(t + 1) * P], wx[n][:], start=True, stop=True)
                    last.then_inc(s["x"], 1)

                def gate_sum(b, par, first=False):
                    if n:
                        return
                    pe.wait_ge(s["gelu"], b + 1)
                    if not first:
                        pe.wait_ge(s["gsum"], b - 1)
                    for t in range(TT):
                        last = pe.matmul(bank[4 + par][0:HID, 0:1], xt[:, par, t, 0:HID], ones[:],
                                         start=(t == 0), stop=(t == TT - 1))
                    last.then_inc(s["gmm"], 1)

                def one(b, par, lag=5):
                    turn(b, par, lag < 2)
                    if lag >= 1:
                        project(b - 1, 1 - par, lag < 3)
                    if lag >= 3:
                        gate_sum(b - 3, 1 - par, lag < 5)

                for b in range(8):
                    one(b, b % 2, min(b, 5))
                with pe.Fori(2, B // 4) as i:
                    for k in range(4):
                        one(4 * i + k, k % 2)
                project(B - 1, 1)
                for b in range(B - 3, B):
                    gate_sum(b, b % 2)

            norm(0)
            pe.wait_ge(norm_s[0]["gsum"], B)
            pe.matmul(bank[6][0:B, 0:H], gsum[:], wg2[:], start=True, stop=True).then_inc(gl_mm, 1)
            phase(pe, 1)

            def attention(l):
                s = att_s[l]

                def proj_tile(b, t):
                    pe.matmul(M[:, 1 - t if l else t, 0:3 * D], ha[:, t * P:(t + 1) * P], wqkv[l][:],
                              start=True, stop=True).then_inc(s["proj"], 1)

                def prep_proj(b):
                    pe.wait_ge(s["h"], b + 1)
                    for t in range(TT):
                        proj_tile(b, t)

                def turn_stack(b, w, bankno):
                    to = M[:, bankno, :].bitcast(F16)
                    for j in range(NJ):
                        for t in range(TT):
                            src = st[:, w, t * H + j * HG:t * H + (j + 1) * HG].rearrange("p h r d -> p (h r d)")
                            last = pe.transpose(to[:, j * T + t * P:j * T + (t + 1) * P], src, ident16[:])
                    last.then_inc(s["sT"], 1)

                def prep_turn(b, drained):
                    pe.wait_ge(s["qkv"], drained)
                    for w in range(2):
                        if l == 0:
                            pe.wait_ge(s["stack"], 2 * b + w + 1)
                        turn_stack(b, w, w)

                def prep_max(b, par, k):
                    if k == 0:
                        pe.wait_ge(s["sE"], 3 * b + 1)
                        pe.wait_ge(s["kE"], b + 1)
                    if k >= 2:
                        pe.wait_ge(s["mred"], 12 * b + k - 1)
                    to, g = M[:, k % 2, :], k % 4
                    if k < 8:
                        v = to.rearrange("p (j k) -> p j k", j=2)
                        pe.matmul(v[:, :, P:T], identb[:], maskQ[:].unsqueeze(1).to_broadcast([P, 2, P]),
                                  start=True, stop=False, skip_group_check=True)
                        js, q0, kn = (2 * (k // 4), 2 * (k // 4) + 1), P, T
                    else:
                        v = to.rearrange("p (j k) -> p j k", j=4)
                        pe.matmul(v[:, :, :], identb[:], maskQ[:].unsqueeze(1).to_broadcast([P, 4, P]),
                                  start=True, stop=False, skip_group_check=True)
                        js, q0, kn = range(4), 0, P
                    for n, j in enumerate(js):
                        last = pe.matmul(v[:, n, :], qsT[32 * g:32 * g + 3 * DH, j, q0:q0 + P],
                                         ksT[32 * g:32 * g + 3 * DH, par, j, 0:kn], start=False, stop=True,
                                         skip_group_check=True, tile_position=(32 * g, 0))
                    last.then_inc(s["mfill"], 1)

                def prep_requeue(b):
                    pe.wait_ge(s["mrow"], b + 1)
                    turn_stack(b, 0, 0)

                def score(b, par, u, first=False):
                    if u == 0:
                        pe.wait_ge(s["sE"], (3 if l else 2) * b + 2)
                    if u in ((0, CH // 2) if l else (0, 1)):
                        pe.wait_ge(s["qz"], 2 * b + (2 if u else 1))
                    if not (first and u < 2):
                        pe.wait_ge(s["exp"], CH * b + u - 1)
                    j = u // 2
                    for i in range(2):
                        g = 2 * (u % 2) + i
                        to = SP[u % 2][:, i, :]
                        for k in range(TT):
                            q0 = P if (l and k) else 0
                            last = pe.matmul(to[:, k * T:k * T + T - q0],
                                             ksT[:, par, j, k * P:(k + 1) * P], qz[:, par, g, j, q0:T],
                                             start=True, stop=True)
                    last.then_inc(s["score"], 1)

                def values(b, par, u, first=False):
                    if u == 0:
                        pe.wait_ge(s["vs"], b + 1)
                    pe.wait_ge(s["sel" if l else "exp"], CH * b + u + 1)
                    if not first and u % 4 == 0:
                        pe.wait_ge(s["o"], 2 * b + u // 4 - 1)
                        if u:
                            pe.wait_ge(s["wr"], b)
                    j = u // 2
                    for k in range(TT):
                        q0 = P if (l and k) else 0
                        for i in range(2):
                            g = 2 * (u % 2) + i
                            c = (j % 2) * T
                            last = pe.matmul(OP[32 * g:32 * g + 32, j // 2, c + q0:c + T],
                                             vs[:, par, k, HG * j + g, :],
                                             pt[:, u % 4, i, k * T:k * T + T - q0],
                                             start=(k == 0), stop=(k == TT - 1),
                                             skip_group_check=True, tile_position=(0, 32 * g))
                    last.then_inc(s["pv"], 1)

                def tail_turn(b, t):
                    if t == 0:
                        pe.wait_ge(s["o"], 2 * b + 2)
                    if t:
                        pe.wait_ge(s["an"], 2 * b + 1)
                    to = OP[:, 1]
                    for j in range(NJ):
                        last = pe.transpose(to[:, j * P:(j + 1) * P], oT[:, j, t * P:(t + 1) * P], ident[:])
                    last.then_inc(s["oT"], 1)

                def tail_an(b):
                    pe.wait_ge(s["an"], 2 * b + 2)
                    to = OP[:, 1]
                    for t in range(TT):
                        last = pe.transpose(to[:, t * P:(t + 1) * P],
                                            an[:, t * H:(t + 1) * H, :].rearrange("p h d -> p (h d)"), ident[:])
                    last.then_inc(s["aT"], 1)

                def tail_wo(b):
                    pe.wait_ge(s["aE"], b + 1)
                    to = OP[:, 1, T:T + TT * D]
                    for t in range(TT):
                        last = pe.matmul(to[:, t * D:(t + 1) * D], aT[:, t * P:(t + 1) * P], wo[l][:],
                                         start=True, stop=True)
                    last.then_inc(s["wo"], 1)

                def one0(b, par, first=False, tail=True, nxt=True, nxt2=True):
                    for u in range(CH):
                        score(b, par, u, first)
                        if tail and u in (2, 3):
                            tail_turn(b - 1, u - 2)
                        if tail and u == 5:
                            tail_wo(b - 1)
                        if tail and u == 0:
                            values(b - 1, 1 - par, CH - 1)
                        if u >= 2:
                            values(b, par, u - 2, first)
                        if tail and u == 4:
                            tail_an(b - 1)
                        if nxt2 and u == 3:
                            pe.wait_ge(s["sE"], 2 * b + 2)
                            prep_proj(b + 2)
                        if nxt and u == 5:
                            prep_turn(b + 1, b + 3 if nxt2 else b + 2)
                    values(b, par, CH - 2, first)

                FILLS = [0, 0, 2, 3, 2, 2, 2, 0]

                def one1(b, par, first=False, tail=True, nxt=True, nxt2=True):
                    done = 0
                    for u in range(CH):
                        if u == CH - 1 and nxt:
                            prep_max(b + 1, 1 - par, 11)
                        score(b, par, u, first)
                        if tail and u == 1:
                            tail_turn(b - 1, 0)
                        if nxt and u == 1:
                            prep_turn(b + 1, b + 2)
                        if u == 2:
                            values(b, par, 0, first)
                        for k in range(done, done + FILLS[u]):
                            if tail and k == 2:
                                tail_turn(b - 1, 1)
                            if tail and k == 4:
                                tail_an(b - 1)
                            if tail and k == 6:
                                tail_wo(b - 1)
                            if nxt:
                                prep_max(b + 1, 1 - par, k)
                        done += FILLS[u]
                        if u > 2:
                            values(b, par, u - 2, first)
                    values(b, par, CH - 2, first)
                    if nxt2:
                        pe.wait_ge(s["h"], b + 3)
                        pe.wait_ge(s["mred"], 12 * (b + 2))
                        proj_tile(b + 2, 0)
                    if nxt:
                        prep_requeue(b + 1)
                    values(b, par, CH - 1, first)
                    if nxt2:
                        pe.wait_ge(s["sE"], 3 * (b + 2))
                        proj_tile(b + 2, 1)

                one = one1 if l else one0
                prep_proj(0)
                if l == 0:
                    pe.wait_ge(s["qkv"], 1)
                    prep_proj(1)
                    prep_turn(0, 2)
                else:
                    prep_turn(0, 1)
                    for k in range(12):
                        prep_max(0, 0, k)
                    pe.wait_ge(s["h"], 2)
                    pe.wait_ge(s["mred"], 12)
                    proj_tile(1, 0)
                    prep_requeue(0)
                    pe.wait_ge(s["sE"], 3)
                    proj_tile(1, 1)
                one(0, 0, True, tail=False)
                one(1, 1)
                with pe.Fori(1, B // 2 - 1) as i:
                    for par in range(2):
                        one(2 * i + par, par)
                one(B - 2, 0, nxt2=False)
                one(B - 1, 1, nxt=False, nxt2=False)
                if l == 0:
                    values(B - 1, 1, CH - 1)
                pe.wait_ge(s["wr"], B - 1)
                tail_turn(B - 1, 0)
                tail_turn(B - 1, 1)
                tail_an(B - 1)
                tail_wo(B - 1)

            def experts(l, E, F):
                s = exp_s[l]
                PARTS = [(0, 0), (0, 1), (1, 0)]

                def weights(g, par, first=False):
                    pe.wait_ge(s["c"], g + 1)
                    if not first:
                        pe.wait_ge(s["done"], g - 2)
                    for t in range(GT):
                        last = pe.transpose(bank[7][0:3 * E, 0:GTOK // 2].bitcast(BF16)[:, t * P:(t + 1) * P],
                                            ccur[l][:, par, t, :], identb[:])
                    last.then_inc(s["cT"], 1)

                def hidden(g, e, first):
                    for f in range(F):
                        k = e * F + f
                        if not (first and k < 4):
                            pe.wait_ge(s["relu"], E * F * g + k - 3)
                        for n, (u, v) in enumerate(PARTS):
                            last = pe.matmul(bank[k % 4], w16[l][:, 0, u, k * P:(k + 1) * P],
                                             h16[:, v, bass.ts(g, GTOK)], start=(n == 0), stop=(n == 2))
                        last.then_inc(s["hid"], 1)

                def row(g, par, e, first):
                    if e == 0:
                        pe.wait_ge(s["cE"], g + 1)
                    if not (first and e == 0):
                        pe.wait_ge(s["rowE"], E * g + e)
                    pe.matmul(bank[6], pick[l][:, e, :], cT3[0:3 * E, par, :],
                              start=True, stop=True).then_inc(s["row"], 1)

                def outputs(g, e, first=False):
                    if not (first and e < 2):
                        pe.wait_ge(s["term"], E * g + e - 1)
                    for f in range(F):
                        k = e * F + f
                        pe.wait_ge(s["lo"], E * F * g + k + 1)
                        for n, (u, v) in enumerate(PARTS):
                            last = pe.matmul(bank[4 + e % 2], w16[l][:, 1, u, k * P:(k + 1) * P],
                                             hid[:, e % 2, f, v, :], start=(f == 0 and n == 0),
                                             stop=(f == F - 1 and n == 2))
                    last.then_inc(s["y"], 1)

                def turn(g, par):
                    pe.wait_ge(s["acc"], (E - 1) * (g + 1))
                    pe.wait_ge(s["cE"], min(g + 3, NG) if isinstance(g, int) else g + 3)
                    for t in range(GT):
                        last = pe.transpose(bank[7][:, t * P:(t + 1) * P], acc[:, par, t * P:(t + 1) * P], ident[:])
                    last.then_inc(s["turn"], 1)

                def one(g, par, prev=True, nxt=True, first=False, head=False):
                    for e in range(E):
                        hidden(g, e, head)
                        row(g, par, e, head)
                        if e:
                            outputs(g, e - 1, head)
                        elif prev:
                            outputs(g - 1, E - 1)
                        if e == 1 and nxt:
                            weights(g + 1, 1 - par, first)
                        if e == 2 and prev:
                            turn(g - 1, 1 - par)

                weights(0, 0, True)
                one(0, 0, prev=False, first=True, head=True)
                one(1, 1, first=True)
                with pe.Fori(1, NG // 2 - 1) as i:
                    for par in range(2):
                        one(2 * i + par, par)
                one(NG - 2, 0)
                one(NG - 1, 1, nxt=False)
                outputs(NG - 1, E - 1)
                turn(NG - 1, 1)

            attention(0)
            phase(pe, 2)
            norm(1)
            phase(pe, 3)
            experts(0, E0, F0)
            phase(pe, 4)
            norm(2)
            phase(pe, 5)
            attention(1)
            phase(pe, 6)
            norm(3)
            phase(pe, 7)
            experts(1, E1, F1)
            phase(pe, 8)


def layout(i):
    import numpy as np

    def c(v):
        return np.ascontiguousarray(v)

    def rep(v, n=P):
        return c(np.broadcast_to(np.asarray(v).reshape(1, -1), (n, np.asarray(v).size)))

    def experts(w, b, w2, b2, e, f):
        return (c(np.transpose(w, (1, 0, 2)).reshape(P, -1)),
                c(np.transpose(np.asarray(w2).reshape(e * f, P, D), (1, 0, 2)).reshape(P, -1)),
                c(np.asarray(b).reshape(e * f, P).T), c(b2.T))

    i = {k: np.asarray(v) for k, v in i.items()}
    a = {"x": c(i["L0_attn_x"])}
    for l in range(2):
        a[f"cT{l}"] = c(i[f"L{l}_c"].T)
        a[f"wmod{l}"] = c(i[f"L{l}_wmod"])
    a["wqkv0"] = c(np.concatenate([i["L0_attn_Wq"].T, i["L0_attn_Wk"].T, i["L0_attn_Wv"].T], axis=1))
    a["wqkv1"] = c(np.concatenate([i["L1_attn_Wq"], i["L1_attn_Wkv"]], axis=1))
    a["wo0"], a["wo1"] = c(i["L0_attn_Wo"].T), c(i["L1_attn_Wo"])
    a["bqkv0"] = rep(np.concatenate([i["L0_attn_bq"], i["L0_attn_bk"], i["L0_attn_bv"]]))
    a["bo0"] = rep(i["L0_attn_bo"])
    a["wx0"], a["bx0"] = c(i["L0_attn_Wg1"].T), rep(i["L0_attn_bg1"])
    a["wx1"] = c(np.concatenate([i["L0_ffn_gate_w"], i["L0_ffn_dp_w1"]], axis=1))
    a["bx1"] = rep(np.concatenate([i["L0_ffn_gate_b"], i["L0_ffn_dp_b1"]]))
    a["wx3"], a["bx3"] = c(i["L1_ffn_Wg"]), rep(i["L1_ffn_bg"])
    a["dpw2"], a["dpb2"] = rep(i["L0_ffn_dp_w2"]), rep(i["L0_ffn_dp_b2"])
    a["wg2"], a["bg2"], a["g"] = c(i["L0_attn_Wg2"].T), rep(i["L0_attn_bg2"], B), rep(i["L0_attn_g"], B)
    a["w1_0"], a["w2_0"], a["b1_0"], a["b2_0"] = experts(
        i["L0_ffn_ew1"], i["L0_ffn_eb1"], i["L0_ffn_ew2"], i["L0_ffn_eb2"], E0, F0)
    a["w1_1"], a["w2_1"], a["b1_1"], a["b2_1"] = experts(
        i["L1_ffn_W1"], i["L1_ffn_b1"], i["L1_ffn_W2"], i["L1_ffn_b2"], E1, F1)
    return a


def kernel(**inputs):
    import concourse.bacc as bacc
    from concourse.bass_utils import run_bass_kernel_spmd

    nc = bacc.Bacc("TRN2", target_bir_lowering=False, num_devices=1)
    arrays = layout(inputs)
    aps = {n: nc.dram_tensor(f"in_{n}", v.shape, F32, kind="ExternalInput").ap() for n, v in arrays.items()}
    out = nc.dram_tensor("out", (B, T, D), F32, kind="ExternalOutput").ap()
    program(nc, aps, out)
    r = run_bass_kernel_spmd(nc, [{f"in_{n}": v for n, v in arrays.items()}], core_ids=[0])
    return r.results[0]["out"]
```
